# Optimizing a Trainium2 kernel written in Bass

```python
import numpy as np
import jax
import jax.numpy as jnp

def _softmax(x, axis=-1):
    return jax.nn.softmax(x, axis=axis)

def _gelu(x):
    return jax.nn.gelu(x, approximate=True)

def _silu(x):
    return jax.nn.silu(x)

def _sigmoid(x):
    return jax.nn.sigmoid(x)

def _layernorm(x, axis=-1, eps=1e-05):
    m = jnp.mean(x, axis=axis, keepdims=True)
    v = jnp.var(x, axis=axis, keepdims=True)
    return (x - m) / jnp.sqrt(v + eps)

def _scatter_add(tgt, idx, src, axis=0):
    return tgt.at[idx].add(src)

def _segment_sum(src, seg, n):
    return jax.ops.segment_sum(src, seg, n)
kernel_name = 'mk_seq_preln_d2_jaxref_r8_fb5670'

def setup_inputs(seed: int=0):
    np.random.seed(seed)
    _w = jnp.asarray

    def _L0_attn_setup():
        import jax, jax.numpy as jnp
        import numpy as np
        import math
        NHEAD = 16
        FACTOR = 5
        key = jax.random.key(seed)
        ks = jax.random.split(key, 10)
        B, L, Dm = (2, 256, 128)
        x = jax.random.normal(ks[0], (B, L, Dm), dtype=jnp.float32)
        w = lambda k: jax.random.normal(k, (Dm, Dm), dtype=jnp.float32) * 0.02
        b = lambda k: jax.random.normal(k, (Dm,), dtype=jnp.float32) * 0.02
        return {'x': x, 'Wq': w(ks[1]), 'bq': b(ks[2]), 'Wk': w(ks[3]), 'bk': b(ks[4]), 'Wv': w(ks[5]), 'bv': b(ks[6]), 'Wo': w(ks[7]), 'bo': b(ks[8])}
    _L0_attn_in = _L0_attn_setup()

    def _L0_ffn_setup():
        import jax, jax.numpy as jnp
        import numpy as np
        CAPACITY_FACTOR = 1.25
        key = jax.random.key(seed)
        k1, k2, k3, k4 = jax.random.split(key, 4)
        B, S, D, E, H = (2, 256, 128, 16, 512)
        inputs = jax.random.normal(k1, (B, S, D), dtype=jnp.float32)
        gate_w = jax.random.normal(k2, (E, D), dtype=jnp.float32) / np.float32(np.sqrt(D))
        w1 = jax.random.normal(k3, (E, D, H), dtype=jnp.float32) / np.float32(np.sqrt(D))
        w2 = jax.random.normal(k4, (E, H, D), dtype=jnp.float32) / np.float32(np.sqrt(H))
        return {'inputs': inputs, 'gate_w': gate_w, 'w1': w1, 'w2': w2}
    _L0_ffn_in = _L0_ffn_setup()

    def _L1_attn_setup():
        import jax, jax.numpy as jnp
        import numpy as np
        from math import sqrt
        EMBED_DIM = 128
        NUM_HEADS = 16
        HEAD_DIM = EMBED_DIM // NUM_HEADS
        SCALE = sqrt(HEAD_DIM)

        def _rotate_half(x):
            x1 = x[..., 0::2]
            x2 = x[..., 1::2]
            return jnp.stack((-x2, x1), axis=-1).reshape(x.shape)

        def _apply_rope(x, seq_len):
            inv_freq = 1.0 / 10000.0 ** (jnp.arange(0, HEAD_DIM, 2, dtype=jnp.float32) / HEAD_DIM)
            pos = jnp.arange(seq_len, dtype=jnp.float32)
            freqs = jnp.outer(pos, inv_freq)
            emb = jnp.concatenate([freqs, freqs], -1)
            cos = jnp.cos(emb)[None, None].astype(x.dtype)
            sin = jnp.sin(emb)[None, None].astype(x.dtype)
            return x * cos + _rotate_half(x) * sin
        key = jax.random.key(seed)
        ks = jax.random.split(key, 9)
        B, S, E = (2, 256, EMBED_DIM)
        s = 1.0 / np.sqrt(E)
        return {'x': jax.random.normal(ks[0], (B, S, E), jnp.float32), 'Wq': jax.random.uniform(ks[1], (E, E), jnp.float32, -s, s), 'bq': jnp.zeros((E,), jnp.float32), 'Wk': jax.random.uniform(ks[2], (E, E), jnp.float32, -s, s), 'bk': jnp.zeros((E,), jnp.float32), 'Wv': jax.random.uniform(ks[3], (E, E), jnp.float32, -s, s), 'bv': jnp.zeros((E,), jnp.float32), 'Wo': jax.random.uniform(ks[4], (E, E), jnp.float32, -s, s), 'bo': jnp.zeros((E,), jnp.float32)}
    _L1_attn_in = _L1_attn_setup()

    def _L1_ffn_setup():
        import jax, jax.numpy as jnp
        import numpy as np
        HIDDEN = 128
        INTER = 512
        key = jax.random.key(seed)
        k1, k2, k3, k4, k5 = jax.random.split(key, 5)
        hidden_states = jax.random.normal(k1, (4, 256, HIDDEN), dtype=jnp.float32)
        W1 = jax.random.normal(k2, (HIDDEN, INTER), dtype=jnp.float32) * (1.0 / np.sqrt(HIDDEN))
        b1 = jax.random.normal(k3, (INTER,), dtype=jnp.float32) * 0.02
        W2 = jax.random.normal(k4, (INTER, HIDDEN), dtype=jnp.float32) * (1.0 / np.sqrt(INTER))
        b2 = jax.random.normal(k5, (HIDDEN,), dtype=jnp.float32) * 0.02
        return {'hidden_states': hidden_states, 'W1': W1, 'b1': b1, 'W2': W2, 'b2': b2}
    _L1_ffn_in = _L1_ffn_setup()
    _d = {'L0_attn_x': _L0_attn_in['x'], 'L0_attn_Wq': _L0_attn_in['Wq'], 'L0_attn_bq': _L0_attn_in['bq'], 'L0_attn_Wk': _L0_attn_in['Wk'], 'L0_attn_bk': _L0_attn_in['bk'], 'L0_attn_Wv': _L0_attn_in['Wv'], 'L0_attn_bv': _L0_attn_in['bv'], 'L0_attn_Wo': _L0_attn_in['Wo'], 'L0_attn_bo': _L0_attn_in['bo'], 'L0_ffn_gate_w': _L0_ffn_in['gate_w'], 'L0_ffn_w1': _L0_ffn_in['w1'], 'L0_ffn_w2': _L0_ffn_in['w2'], 'L1_attn_Wq': _L1_attn_in['Wq'], 'L1_attn_bq': _L1_attn_in['bq'], 'L1_attn_Wk': _L1_attn_in['Wk'], 'L1_attn_bk': _L1_attn_in['bk'], 'L1_attn_Wv': _L1_attn_in['Wv'], 'L1_attn_bv': _L1_attn_in['bv'], 'L1_attn_Wo': _L1_attn_in['Wo'], 'L1_attn_bo': _L1_attn_in['bo'], 'L1_ffn_W1': _L1_ffn_in['W1'], 'L1_ffn_b1': _L1_ffn_in['b1'], 'L1_ffn_W2': _L1_ffn_in['W2'], 'L1_ffn_b2': _L1_ffn_in['b2']}
    _x0 = _d['L0_attn_x']
    _d['L0_attn_x'] = jax.random.normal(jax.random.fold_in(jax.random.key(seed), 1), (8, 256, 128), dtype=_x0.dtype)
    del _x0
    return _d

def reference(L0_attn_x, L0_attn_Wq, L0_attn_bq, L0_attn_Wk, L0_attn_bk, L0_attn_Wv, L0_attn_bv, L0_attn_Wo, L0_attn_bo, L0_ffn_gate_w, L0_ffn_w1, L0_ffn_w2, L1_attn_Wq, L1_attn_bq, L1_attn_Wk, L1_attn_bk, L1_attn_Wv, L1_attn_bv, L1_attn_Wo, L1_attn_bo, L1_ffn_W1, L1_ffn_b1, L1_ffn_W2, L1_ffn_b2):

    def _L0_attn_ref(x, Wq, bq, Wk, bk, Wv, bv, Wo, bo):
        import jax, jax.numpy as jnp
        import numpy as np
        import math
        NHEAD = 16
        FACTOR = 5
        B, L, Dm = x.shape
        H = NHEAD
        D = Dm // H
        U = min(L, int(FACTOR * math.log(L)) if L > 1 else L)

        def proj(W, b):
            return (x @ W.T + b).reshape(B, L, H, D).transpose(0, 2, 1, 3)
        Q = proj(Wq, bq)
        K = proj(Wk, bk)
        V = proj(Wv, bv)
        scores = jnp.einsum('bhqd,bhkd->bhqk', Q, K) / math.sqrt(D)
        thresh = jax.lax.top_k(scores, U)[0][..., -1:]
        scores = jnp.where(scores < thresh, -jnp.inf, scores)
        attn = jax.nn.softmax(scores, axis=-1)
        context = jnp.einsum('bhqk,bhkd->bhqd', attn, V)
        context = context.transpose(0, 2, 1, 3).reshape(B, L, Dm)
        return context @ Wo.T + bo

    def _L0_ffn_ref(inputs, gate_w, w1, w2):
        import jax, jax.numpy as jnp
        import numpy as np
        CAPACITY_FACTOR = 1.25
        orig_shape = inputs.shape
        D = orig_shape[-1]
        tokens = inputs.reshape(-1, D)
        T = tokens.shape[0]
        E = gate_w.shape[0]
        C = int(CAPACITY_FACTOR * T / E)
        logits = tokens @ gate_w.T
        probs = jax.nn.softmax(logits, axis=-1)
        expert_idx = jnp.argmax(probs, axis=-1)
        mask = jax.nn.one_hot(expert_idx, E, dtype=jnp.int32)
        locations = jnp.cumsum(mask, axis=0) - 1
        mask = mask * (locations < C)
        loc_oh = jax.nn.one_hot(locations, C, dtype=probs.dtype)
        sec_mask = mask[:, :, None].astype(probs.dtype) * loc_oh
        combine_weights = probs[:, :, None] * sec_mask
        dispatch = jnp.einsum('tec,td->ecd', sec_mask, tokens)
        h = jax.nn.relu(jnp.einsum('ecd,edh->ech', dispatch, w1))
        expert_out = jnp.einsum('ech,ehd->ecd', h, w2)
        ans = jnp.einsum('tec,ecd->td', combine_weights, expert_out)
        return ans.reshape(orig_shape)

    def _L1_attn_ref(x, Wq, bq, Wk, bk, Wv, bv, Wo, bo):
        import jax, jax.numpy as jnp
        import numpy as np
        from math import sqrt
        EMBED_DIM = 128
        NUM_HEADS = 16
        HEAD_DIM = EMBED_DIM // NUM_HEADS
        SCALE = sqrt(HEAD_DIM)

        def _rotate_half(x):
            x1 = x[..., 0::2]
            x2 = x[..., 1::2]
            return jnp.stack((-x2, x1), axis=-1).reshape(x.shape)

        def _apply_rope(x, seq_len):
            inv_freq = 1.0 / 10000.0 ** (jnp.arange(0, HEAD_DIM, 2, dtype=jnp.float32) / HEAD_DIM)
            pos = jnp.arange(seq_len, dtype=jnp.float32)
            freqs = jnp.outer(pos, inv_freq)
            emb = jnp.concatenate([freqs, freqs], -1)
            cos = jnp.cos(emb)[None, None].astype(x.dtype)
            sin = jnp.sin(emb)[None, None].astype(x.dtype)
            return x * cos + _rotate_half(x) * sin
        B, S, E = x.shape
        H, D = (NUM_HEADS, HEAD_DIM)
        q = (x @ Wq.T + bq).reshape(B, S, H, D).transpose(0, 2, 1, 3)
        k = (x @ Wk.T + bk).reshape(B, S, H, D).transpose(0, 2, 1, 3)
        v = (x @ Wv.T + bv).reshape(B, S, H, D).transpose(0, 2, 1, 3)
        q = _apply_rope(q, S)
        k = _apply_rope(k, S)
        attn = jnp.einsum('bhqd,bhkd->bhqk', q, k) / SCALE
        attn = jax.nn.softmax(attn, axis=-1)
        out = jnp.einsum('bhqk,bhkd->bhqd', attn, v)
        out = out.transpose(0, 2, 1, 3).reshape(B, S, E)
        return out @ Wo.T + bo

    def _L1_ffn_ref(hidden_states, W1, b1, W2, b2):
        import jax, jax.numpy as jnp
        import numpy as np
        HIDDEN = 128
        INTER = 512
        h = jax.nn.relu(jnp.einsum('bsh,hi->bsi', hidden_states, W1) + b1)
        return jnp.einsum('bsi,ih->bsh', h, W2) + b2
    x = L0_attn_x
    x = x + _L0_attn_ref(_layernorm(x, axis=-1), L0_attn_Wq, L0_attn_bq, L0_attn_Wk, L0_attn_bk, L0_attn_Wv, L0_attn_bv, L0_attn_Wo, L0_attn_bo)
    x = x + _L0_ffn_ref(_layernorm(x, axis=-1), L0_ffn_gate_w, L0_ffn_w1, L0_ffn_w2)
    x = x + _L1_attn_ref(_layernorm(x, axis=-1), L1_attn_Wq, L1_attn_bq, L1_attn_Wk, L1_attn_bk, L1_attn_Wv, L1_attn_bv, L1_attn_Wo, L1_attn_bo)
    x = x + _L1_ffn_ref(_layernorm(x, axis=-1), L1_ffn_W1, L1_ffn_b1, L1_ffn_W2, L1_ffn_b2)
    return x

_drawn_inputs = setup_inputs


def setup_inputs(seed=0):
    import zlib

    import numpy as np

    out = dict(_drawn_inputs(seed))
    spreads = {'L1_attn_bq': (0.0, 0.8),
     'L1_attn_bk': (0.0, 0.8),
     'L1_attn_bv': (0.0, 0.1),
     'L1_attn_bo': (0.0, 0.1)}
    factors = {'L0_attn_Wq': 2.982,
     'L0_attn_bq': 7.428,
     'L0_attn_Wk': 3.222,
     'L0_attn_bk': 8.0,
     'L0_attn_Wv': 3.04,
     'L0_attn_bv': 6.004,
     'L0_attn_Wo': 2.82,
     'L1_attn_Wq': 4.745,
     'L1_attn_Wk': 4.565,
     'L1_ffn_b1': 5.121,
     'L1_ffn_b2': 3.49}
    for name, (base, spread) in spreads.items():
        noise = np.random.default_rng([zlib.crc32(name.encode()), seed]).standard_normal(out[name].shape)
        drawn = base * np.exp(spread * noise) if base else spread * noise
        out[name] = jnp.asarray(drawn.astype(out[name].dtype))
    for name, factor in factors.items():
        out[name] = (out[name] * factor).astype(out[name].dtype)
    return out
```

```python
from contextlib import ExitStack

import concourse.bass as bass
from concourse import mybir

F32 = mybir.dt.float32
BF16 = mybir.dt.bfloat16
U32 = mybir.dt.uint32
ALU = mybir.AluOpType
ACT = mybir.ActivationFunctionType
AX_X = mybir.AxisListType.X

P = 128
BATCH, SEQ, DM = 8, 256, 128
HEADS = 16
HD = DM // HEADS
HV = HD + 1
TILES = BATCH * SEQ // P
TOKENS = TILES * P
CH = 4
CHUNKS = TILES // CH
CT = CH * P
KT = SEQ // P
GROUPS = 4
JH = HEADS // GROUPS
ITERS = BATCH * GROUPS
VW = JH * HV
TOPU = 27
ROUNDS = 4
SCALE = HD ** -0.5
EPS = 1e-5
NEG = -3.0e38
EXPERTS, HID = 16, 512
HC = HID // P
CAP = 160
CAPH = CAP // 2
SLOTS = EXPERTS * CAP
RING = 8
XB = 4
ER = TILES * EXPERTS


def build(nc, x, w0, bqk0, bv0, bo0, gate, w1, w2, w5, bqk1, bv1, bo1, ffw1, ffb1, ffw2, ffb2,
          ident_d, hmask_d, cos_d, sin_d, triu_d, rev_d, spill_d, out):
    with ExitStack() as ctx:
        def sb(name, shape, dt=F32):
            return ctx.enter_context(nc.sbuf_tensor(name, shape, dt))

        def sem(name):
            return ctx.enter_context(nc.semaphore(name))

        def pair(name):
            return [sem(f"{name}0"), sem(f"{name}1")]

        dispatched = nc.dram_tensor("dispatched", (SLOTS + TOKENS, DM), F32, kind="Internal").ap()
        expert_out = nc.dram_tensor("expert_out", (SLOTS, DM), F32, kind="Internal").ap()

        ident = sb("ident", [P, P])
        ones_row = sb("ones_row", [1, P])
        neg_half = sb("neg_half", [P, TILES])
        hmask = sb("hmask", [P, HEADS])
        wqkvo = [sb("wqkvo0", [P, 4, DM]), sb("wqkvo1", [P, 6, DM])]
        bqk = [sb("bqk0_sb", [P, 2]), sb("bqk1_sb", [P, 4])]
        bv_b = [sb("bv0_sb", [P, DM]), sb("bv1_sb", [P, DM])]
        bo_row = [sb("bo0_sb", [1, DM]), sb("bo1_sb", [1, DM])]
        cos_t = sb("cos_t", [P, CT])
        sin_t = sb("sin_t", [P, CT])
        gate_sb = sb("gate_sb", [P, EXPERTS])
        triu = sb("triu", [P, P])
        zero_rows = sb("zero_rows", [P, DM])
        triu_b = sb("triu_b", [P, P], BF16)
        ones_b = sb("ones_b", [P, P], BF16)
        rev = sb("rev", [P, TILES, EXPERTS])
        spill = sb("spill", [P, TILES])
        ffw1_sb = sb("ffw1_sb", [P, HID])
        ffw2_sb = sb("ffw2_sb", [P, HC, DM])
        ffb1_sb = sb("ffb1_sb", [P, HC])
        ffb2_row = sb("ffb2_row", [1, DM])
        w1_ring = sb("w1_ring", [P, RING, HID])
        w2_ring = sb("w2_ring", [P, RING, HC, DM])
        x_sb = sb("x_sb", [P, TILES, DM])
        xn_all = sb("xn_all", [P, TILES, DM])
        stats = sb("stats", [P, TILES, 6])
        ln_t = sb("ln_t", [P, 6, TILES])
        ln_mean = sb("ln_mean", [P, TILES])
        ln_rstd = sb("ln_rstd", [P, TILES])
        stage = sb("stage", [P, CH, DM])
        stageT = sb("stageT", [P, CT])
        rope_t = sb("rope_t", [P, 2, 2, CT])
        qk_all = sb("qk_all", [P, 2, TOKENS])
        q_st = sb("q_st", [P, JH, SEQ])
        v_all = sb("v_all", [P, TILES, GROUPS, VW])
        v_st = sb("v_st", [P, KT, JH, 32])
        ot_sb = sb("ot_sb", [P, SEQ])
        top = sb("top", [P, 4, 8 * ROUNDS])
        rest = sb("rest", [P, 4, SEQ])
        negm = sb("negm", [P, 2, 4])
        s_sb = sb("s_sb", [P, 2, 4, SEQ])
        e_sb = sb("e_sb", [P, 2, 4, SEQ])
        pt_sb = sb("pt_sb", [P, 2, KT, SEQ])
        recip = sb("recip", [P, KT, JH])
        hT = sb("hT", [P, HC, CT])
        logits = sb("logits", [P, TILES, EXPERTS])
        rt = sb("rt", [P, 4, TILES, EXPERTS])
        mask_b = sb("mask_b", [P, TILES, EXPERTS], BF16)
        rs = sb("rs", [P, 12, TILES])
        slot_idx = sb("slot_idx", [P, TILES], U32)
        back_idx = sb("back_idx", [P, TILES], U32)
        xg = sb("xg", [CAPH, 2, XB * 2, DM])
        y_sb = sb("y_sb", [CAPH, RING, 2, DM])
        ehT = sb("ehT", [P, 2, HC, CAP])
        xeT = sb("xeT", [P, 2, CAP])

        ps = ctx.enter_context(nc.psum_tensor("ps", [P, 8, 512], F32))

        x_in, consts_in, late_in, route_in, ff_in = sem("x_in"), sem("consts_in"), sem("late_in"), sem("route_in"), sem("ff_in")
        setup_done = sem("setup_done")
        setup_dve = sem("setup_dve")
        stats_done = sem("stats_done")
        ln_step = sem("ln_step")
        rstd_done = sem("rstd_done")
        normed = sem("normed")
        stage_T = sem("stage_T")
        stageT_done = sem("stageT_done")
        proj_done = pair("proj_done")
        q_saved, k_saved, v_saved = pair("q_saved"), pair("k_saved"), pair("v_saved")
        rope_step, rope_q = sem("rope_step"), sem("rope_q")
        q_staged, v_staged = pair("q_staged"), pair("v_staged")
        scores_done = pair("scores_done")
        top_step = sem("top_step")
        max_done = sem("max_done")
        neg_done = pair("neg_done")
        exp_done = pair("exp_done")
        scores_saved = sem("scores_saved")
        probs_done = sem("probs_done")
        probs_T = pair("probs_T")
        pt_done = pair("pt_done")
        pv_done = pair("pv_done")
        ot_saved = pair("ot_saved")
        ctx_T = pair("ctx_T")
        recip_done, ctx_done = pair("recip_done"), pair("ctx_done")
        ctx_staged = pair("ctx_staged")
        out_done, res_done = pair("out_done"), pair("res_done")
        rows_kept = sem("rows_kept")
        logits_done, logits_saved = sem("logits_done"), sem("logits_saved")
        rstep = sem("rstep")
        gate_exp = sem("gate_exp")
        mask_done = sem("mask_done")
        cum_done = sem("cum_done")
        slots_ready = sem("slots_ready")
        zeroed = sem("zeroed")
        scattered = sem("scattered")
        xg_in = [sem(f"xg_in{s}") for s in range(2)]
        w_in = [sem(f"w_in{r}") for r in range(RING)]
        w_again = [sem(f"w_again{r}") for r in range(RING)]
        xe_T, xeT_done = sem("xe_T"), sem("xeT_done")
        eh_done, relu_done = sem("eh_done"), sem("relu_done")
        ey_done, y_saved = sem("ey_done"), sem("y_saved")
        y_out = sem("y_out")
        gathered = sem("gathered")
        moe_added = sem("moe_added")
        h_done, h_saved_a, h_saved_v = sem("h_done"), sem("h_saved_a"), sem("h_saved_v")
        ff_done, added = sem("ff_done"), sem("added")
        stored = sem("stored")

        block = ctx.enter_context(nc.Block())

        ps_T = ps[:, 0, :]
        ps_q, ps_k, ps_v, ps_qr, ps_kr = (ps[:, i, :] for i in range(1, 6))
        ps_out = ps[:, 1, :]

        def ps_scores(hp):
            return ps[:, 2 * hp:2 * hp + 2, :].rearrange("p a (b n) -> p (a b) n", b=KT)

        ps_o = ps[:, 6, 0:SEQ]
        ps_ctx = ps[:, 7, 0:SEQ]

        USE = {"qkv0": 0, "out0": 1, "moe": 2, "qkv1": 3, "out1": 4, "mlp": 5}
        NORMS = {"qkv0": 0, "moe": 1, "qkv1": 2, "mlp": 3}

        @block.sync
        def _(sp):
            sp.dma_start(x_sb[:], x.rearrange("b (t p) d -> p (b t) d", p=P)).then_inc(x_in, 16)
            for dst, src in ((ident[:], ident_d), (hmask[:], hmask_d), (wqkvo[0][:], w0), (bqk[0][:], bqk0),
                             (bv_b[0][:], bv0.partition_broadcast(P)), (bo_row[0][:], bo0)):
                sp.dma_start(dst, src).then_inc(consts_in, 16)
            for dst, src in ((wqkvo[1][:], w5), (bqk[1][:], bqk1), (bv_b[1][:], bv1.partition_broadcast(P)),
                             (bo_row[1][:], bo1), (cos_t[:], cos_d), (sin_t[:], sin_d)):
                sp.dma_start(dst, src).then_inc(late_in, 16)
            for dst, src in ((gate_sb[:], gate), (triu[:], triu_d), (rev[:], rev_d), (spill[:], spill_d)):
                sp.dma_start(dst, src).then_inc(route_in, 16)
            for dst, src in ((ffw1_sb[:], ffw1), (ffw2_sb[:], ffw2.rearrange("(c p) d -> p c d", p=P)),
                             (ffb1_sb[:], ffb1), (ffb2_row[:], ffb2)):
                sp.dma_start(dst, src).then_inc(ff_in, 16)
            for r in range(RING):
                sp.dma_start(w1_ring[:, r, :], w1[r]).then_inc(w_in[r], 16)
                sp.dma_start(w2_ring[:, r], w2[r].rearrange("(c p) d -> p c d", p=P)).then_inc(w_in[r], 16)
            sp.wait_ge(setup_dve, 2)
            sp.dma_start(dispatched[0:SLOTS, :].rearrange("(a p) d -> p a d", p=P), zero_rows[:].unsqueeze(1).to_broadcast([P, SLOTS // P, DM])).then_inc(zeroed, 16)
            sp.wait_ge(scattered, 16 * TILES)

            def load_rows(i, s):
                e0 = i * RING + s * XB
                sp.dma_start(xg[:, s], dispatched[bass.ds(e0 * CAP, XB * CAP), :].rearrange("(a p) d -> p a d", p=CAPH))\
                    .then_inc(xg_in[s], 16)

            def store_rows(i, r):
                e = i * RING + r
                sp.wait_ge(y_saved, i * RING + r + 1)
                sp.dma_start(expert_out[bass.ds(e * CAP, CAP), :].rearrange("(a p) d -> p a d", p=CAPH), y_sb[:, r])\
                    .then_inc(y_out, 16)

            load_rows(0, 0)
            load_rows(0, 1)
            for r in range(RING):
                store_rows(0, r)
                if r % XB == XB - 1:
                    load_rows(1, r // XB)
            for r in range(RING):
                store_rows(1, r)
            with sp.Fori(0, CHUNKS) as c:
                sp.wait_ge(added, c + 1)
                sp.dma_start(out.rearrange("b (t p) d -> p (b t) d", p=P)[:, bass.ds(c * CH, CH), :],
                             x_sb[:, bass.ds(c * CH, CH), :]).then_inc(stored, 16)
            sp.wait_ge(stored, 16 * CHUNKS)

        @block.gpsimd
        def _(pool):
            nc.gpsimd.memset(ones_row[:], 1.0).then_inc(setup_done, 1)
            nc.gpsimd.memset(neg_half[:], -0.5).then_inc(setup_done, 1)
            nc.gpsimd.memset(v_st[:], 0.0).then_inc(setup_done, 1)
            nc.gpsimd.memset(v_all[:], 1.0).then_inc(setup_done, 1)

            def rstd(n):
                pool.wait_ge(ln_step, 8 * (n + 1))
                if n == 0:
                    pool.wait_ge(setup_done, 2)
                nc.gpsimd.tensor_tensor(ln_rstd[:], ln_t[:, 5, :], neg_half[:], ALU.pow).then_inc(rstd_done, 1)

            def stage_heads(L, it):
                b, g = it // GROUPS, it % GROUPS
                if it is not first:
                    pool.wait_ge(scores_done[L], 2 * it)
                q = qk_all[:, 0, bass.ds(b * SEQ, SEQ)].unsqueeze(1).to_broadcast([P, JH, SEQ])
                m = hmask[:, bass.ds(g * JH, JH)].unsqueeze(2).to_broadcast([P, JH, SEQ])
                nc.gpsimd.tensor_tensor(q_st[:], q, m, ALU.mult).then_inc(q_staged[L], 1)
                if it is not first:
                    pool.wait_ge(pv_done[L], 2 * it)
                nc.gpsimd.tensor_copy(
                    v_st[:, :, :, 0:HV],
                    v_all[:, bass.ds(b * KT, KT), bass.ds(g, 1), :].rearrange("p t a (j d) -> p t (a j) d", d=HV),
                ).then_inc(v_staged[L], 1)

            first = 0

            def stage_all(L):
                pool.wait_ge(q_saved[L], CHUNKS)
                pool.wait_ge(v_saved[L], TILES)
                if L == 0:
                    pool.wait_ge(setup_done, 4)
                    pool.wait_ge(consts_in, 16 * 6)
                stage_heads(L, first)
                with pool.Fori(1, ITERS) as it:
                    stage_heads(L, it)

            rstd(0)
            stage_all(0)
            rstd(1)
            with pool.Fori(0, CHUNKS) as c:
                pool.wait_ge(normed, (CHUNKS + c + 1) * CH)
                nc.gpsimd.tensor_copy(xn_all[:, bass.ds(c * CH, CH), :], stage[:]).then_inc(rows_kept, 1)
            pool.wait_ge(slots_ready, 2)
            pool.wait_ge(zeroed, 16)
            pool.wait_ge(rows_kept, CHUNKS)
            for t in range(TILES):
                pool.indirect_dma_start(dispatched[:, :], bass.IndirectOffsetOnAxis(slot_idx[:, t:t + 1], 0),
                                        xn_all[:, t, :], None).then_inc(scattered, 16)
            for r in range(RING):
                pool.wait_ge(ey_done, r + 1)
                pool.dma_start(w1_ring[:, r, :], w1[RING + r]).then_inc(w_again[r], 16)
                pool.dma_start(w2_ring[:, r], w2[RING + r].rearrange("(c p) d -> p c d", p=P)).then_inc(w_again[r], 16)
            pool.wait_ge(y_out, 16 * EXPERTS)
            pool.wait_ge(scattered, 16 * TILES)
            for t in range(TILES):
                pool.indirect_dma_start(xn_all[:, t, :], None, expert_out[:, :],
                                        bass.IndirectOffsetOnAxis(back_idx[:, t:t + 1], 0)).then_inc(gathered, 16)
            rstd(2)
            stage_all(1)
            rstd(3)

        @block.scalar
        def _(act):
            def save_T(use, c):
                k = USE[use] * CHUNKS
                act.wait_ge(stage_T, k + c + 1)
                nc.scalar.activation(stageT[:], ps_T, ACT.Copy).then_inc(stageT_done, 1)

            def qkv0(c):
                save_T("qkv0", c)
                act.wait_ge(proj_done[0], 3 * c + 1)
                nc.scalar.activation(qk_all[:, 0, bass.ds(c * CT, CT)], ps_q, ACT.Identity, bias=bqk[0][:, 0:1]).then_inc(q_saved[0], 1)

            def qkv1(c):
                save_T("qkv1", c)
                for i, p in enumerate((ps_q, ps_qr)):
                    act.wait_ge(proj_done[1], 5 * c + 1 + i)
                    nc.scalar.activation(rope_t[:, i, 0, :], p, ACT.Identity, bias=bqk[1][:, 2 * i:2 * i + 1]).then_inc(rope_q, 1)

            def exps(L, it, hp):
                n = 2 * it + hp
                act.wait_ge(neg_done[L], n + 1)
                if it is not first:
                    act.wait_ge(probs_T[L], 2 * (2 * it + hp - 2) + 2)
                src = s_sb[:, hp] if L == 0 else ps_scores(hp)
                for u in range(4):
                    nc.scalar.activation(e_sb[:, hp, u, :], src[:, u, :], ACT.Exp,
                                         bias=negm[:, hp, u:u + 1], scale=SCALE).then_inc(exp_done[L], 1)

            def save_scores(it, hp):
                act.wait_ge(scores_done[0], 2 * it + hp + 1)
                if it is not first:
                    act.wait_ge(probs_done, 4 * (2 * it + hp - 1))
                nc.scalar.activation(s_sb[:, hp], ps_scores(hp), ACT.Copy).then_inc(scores_saved, 1)

            def save_pt(L, it, hp, jj):
                act.wait_ge(probs_T[L], 2 * (2 * it + hp) + jj + 1)
                if not (it is first and hp == 0):
                    act.wait_ge(pv_done[L], 2 * it + hp)
                nc.scalar.activation(pt_sb[:, jj].rearrange("p a n -> p (a n)"), ps[:, 4 + jj, :], ACT.Copy).then_inc(pt_done[L], 1)

            def save_ot(L, it):
                act.wait_ge(pv_done[L], 2 * it + 2)
                if it is not first:
                    act.wait_ge(ctx_T[L], it)
                nc.scalar.activation(ot_sb[:], ps_o, ACT.Copy).then_inc(ot_saved[L], 1)

            first = 0

            def attention(L):
                def step(it, prev, last=False):
                    exps(L, it, 0)
                    if L == 0:
                        save_scores(it, 1)
                    if prev is not None:
                        save_pt(L, prev, 1, 0)
                        save_pt(L, prev, 1, 1)
                        save_ot(L, prev)
                    exps(L, it, 1)
                    if L == 0 and not last:
                        save_scores(it + 1, 0)
                    save_pt(L, it, 0, 0)
                    save_pt(L, it, 0, 1)

                if L == 0:
                    save_scores(first, 0)
                step(first, None)
                step(1, first)
                with act.Fori(2, ITERS - 1) as it:
                    step(it, it - 1)
                step(ITERS - 1, ITERS - 2, last=True)
                save_pt(L, ITERS - 1, 1, 0)
                save_pt(L, ITERS - 1, 1, 1)
                save_ot(L, ITERS - 1)

            act.wait_ge(consts_in, 16 * 6)
            with act.Fori(0, CHUNKS) as c:
                qkv0(c)
            attention(0)
            with act.Fori(0, CHUNKS) as c:
                save_T("out0", c)
            with act.Fori(0, CHUNKS) as c:
                save_T("moe", c)
                act.wait_ge(logits_done, c + 1)
                nc.scalar.activation(logits[:, bass.ds(c * CH, CH), :], ps[:, 1, 0:CH * EXPERTS].rearrange("p (t e) -> p t e", e=EXPERTS),
                                     ACT.Copy).then_inc(logits_saved, 1)
            act.wait_ge(rstep, 2)
            nc.scalar.activation(rt[:, 1], rt[:, 0], ACT.Exp).then_inc(gate_exp, 1)
            for e in range(EXPERTS):
                act.wait_ge(xe_T, e + 1)
                if e >= 2:
                    act.wait_ge(eh_done, 2 * (e - 2) + 2)
                nc.scalar.activation(xeT[:, e % 2, :], ps[:, e % 2, 0:CAP], ACT.Copy).then_inc(xeT_done, 1)
                if e >= 1:
                    act.wait_ge(ey_done, e)
                    if e - 1 >= RING:
                        act.wait_ge(y_out, 16 * (e - RING))
                    nc.scalar.activation(y_sb[:, (e - 1) % RING].rearrange("p a d -> p (a d)"),
                                         ps[0:CAPH, 6 + (e - 1) % 2, 0:2 * DM], ACT.Copy).then_inc(y_saved, 1)
            act.wait_ge(ey_done, EXPERTS)
            act.wait_ge(y_out, 16 * (EXPERTS - RING))
            nc.scalar.activation(y_sb[:, RING - 1].rearrange("p a d -> p (a d)"),
                                 ps[0:CAPH, 7, 0:2 * DM], ACT.Copy).then_inc(y_saved, 1)
            act.wait_ge(late_in, 16 * 6)
            qkv1(0)
            with act.Fori(1, CHUNKS) as c:
                act.wait_ge(rope_step, 6 * c)
                qkv1(c)
            attention(1)
            with act.Fori(0, CHUNKS) as c:
                save_T("out1", c)
            act.wait_ge(ff_in, 16 * 4)
            with act.Fori(0, CHUNKS) as c:
                save_T("mlp", c)
                for i in range(2):
                    act.wait_ge(h_done, HC * c + i + 1)
                    nc.scalar.activation(hT[:, i, :], ps[:, 2 + i, :], ACT.Relu, bias=ffb1_sb[:, i:i + 1]).then_inc(h_saved_a, 1)

        @block.tensor
        def _(pe):
            def transpose_chunk(use, c, ready, count):
                k = USE[use] * CHUNKS
                if not (use == "qkv0" and c is first):
                    pe.wait_ge(stageT_done, k + c)
                pe.wait_ge(ready, count)
                for t in range(CH):
                    mm = nc.tensor.transpose(ps_T[:, t * P:(t + 1) * P], stage[:, t, :], ident[:])
                mm.then_inc(stage_T, 1)
                pe.wait_ge(stageT_done, k + c + 1)

            first = 0

            def qkv(L, c):
                transpose_chunk(f"qkv{L}", c, normed, NORMS[f"qkv{L}"] * TILES + CH * c + CH)
                w = wqkvo[L]
                if c is not first:
                    pe.wait_ge(q_saved[L], c)
                    pe.wait_ge(k_saved[L], c)
                    pe.wait_ge(v_saved[L], CH * c)
                nc.tensor.matmul(ps_q, w[:, 0, :], stageT[:], start=True, stop=True).then_inc(proj_done[L], 1)
                if L == 1:
                    nc.tensor.matmul(ps_qr, w[:, 4, :], stageT[:], start=True, stop=True).then_inc(proj_done[L], 1)
                nc.tensor.matmul(ps_k, w[:, 1, :], stageT[:], start=True, stop=True).then_inc(proj_done[L], 1)
                if L == 1:
                    nc.tensor.matmul(ps_kr, w[:, 5, :], stageT[:], start=True, stop=True).then_inc(proj_done[L], 1)
                for t in range(CH):
                    mm = nc.tensor.matmul(ps_v[:, t * P:(t + 1) * P], stageT[:, t * P:(t + 1) * P], w[:, 2, :], start=True, stop=True)
                mm.then_inc(proj_done[L], 1)

            weights_ready = [probs_done, exp_done[1]]
            scores_read, per_half = [scores_saved, exp_done[1]], [1, 4]

            def scores(L, it, hp):
                if hp == 0:
                    pe.wait_ge(q_staged[L], it + 1)
                if it is not first:
                    pe.wait_ge(scores_read[L], per_half[L] * (2 * it + hp - 1))
                b = it // GROUPS
                for jj in range(2):
                    for qt in range(KT):
                        mm = nc.tensor.matmul(ps_scores(hp)[:, 2 * jj + qt, :], q_st[:, 2 * hp + jj, qt * P:(qt + 1) * P],
                                              qk_all[:, 1, bass.ds(b * SEQ, SEQ)], start=True, stop=True)
                mm.then_inc(scores_done[L], 1)

            def weigh(L, it, hp):
                n = 2 * it + hp
                for jj in range(2):
                    pe.wait_ge(weights_ready[L], 4 * n + 2 * jj + 2)
                    if not (it is first and hp == 0):
                        pe.wait_ge(pt_done[L], 2 * n + jj - 1)
                    for kt in range(KT):
                        for qt in range(KT):
                            mm = nc.tensor.transpose(ps[:, 4 + jj, kt * SEQ + qt * P:kt * SEQ + (qt + 1) * P],
                                                     e_sb[:, hp, 2 * jj + qt, kt * P:(kt + 1) * P], ident[:])
                    mm.then_inc(probs_T[L], 1)
                if hp == 0:
                    pe.wait_ge(v_staged[L], it + 1)
                    if it is not first:
                        pe.wait_ge(ot_saved[L], it)
                for jj in range(2):
                    j = 2 * hp + jj
                    pe.wait_ge(pt_done[L], 2 * n + jj + 1)
                    for kt in range(KT):
                        mm = nc.tensor.matmul(ps_o[32 * j:32 * j + 32, :], v_st[:, kt, j, :], pt_sb[:, jj, kt, :],
                                              start=(kt == 0), stop=(kt == KT - 1), skip_group_check=True)
                mm.then_inc(pv_done[L], 1)

            def turn_back(L, it):
                pe.wait_ge(ot_saved[L], it + 1)
                if it is not first:
                    pe.wait_ge(ctx_done[L], it)
                for qt in range(KT):
                    mm = nc.tensor.transpose(ps_ctx[:, qt * P:(qt + 1) * P], ot_sb[:, qt * P:(qt + 1) * P], ident[:])
                mm.then_inc(ctx_T[L], 1)

            def attention(L):
                scores(L, first, 0)
                scores(L, first, 1)
                scores(L, 1, 0)
                weigh(L, first, 0)
                scores(L, 1, 1)
                weigh(L, first, 1)
                scores(L, 2, 0)
                turn_back(L, first)
                weigh(L, 1, 0)
                scores(L, 2, 1)
                weigh(L, 1, 1)
                with pe.Fori(3, ITERS) as it:
                    scores(L, it, 0)
                    turn_back(L, it - 2)
                    weigh(L, it - 1, 0)
                    scores(L, it, 1)
                    weigh(L, it - 1, 1)
                turn_back(L, ITERS - 2)
                weigh(L, ITERS - 1, 0)
                weigh(L, ITERS - 1, 1)
                turn_back(L, ITERS - 1)

            def project(L, c):
                transpose_chunk(f"out{L}", c, ctx_staged[L], c + 1)
                if c is not first:
                    pe.wait_ge(res_done[L], c)
                for t in range(CH):
                    nc.tensor.matmul(ps_out[:, t * P:(t + 1) * P], stageT[:, t * P:(t + 1) * P], wqkvo[L][:, 3, :], start=True, stop=False)
                    mm = nc.tensor.matmul(ps_out[:, t * P:(t + 1) * P], ones_row[:], bo_row[L][:], start=False, stop=True)
                mm.then_inc(out_done[L], 1)

            pe.wait_ge(consts_in, 16 * 6)
            pe.wait_ge(setup_done, 1)
            qkv(0, first)
            with pe.Fori(1, CHUNKS) as c:
                qkv(0, c)
            pe.wait_ge(q_saved[0], CHUNKS)
            pe.wait_ge(k_saved[0], CHUNKS)
            pe.wait_ge(v_saved[0], TILES)
            attention(0)
            project(0, first)
            with pe.Fori(1, CHUNKS) as c:
                project(0, c)

            pe.wait_ge(route_in, 16 * 4)
            pe.wait_ge(res_done[0], CHUNKS)

            def gates(c):
                transpose_chunk("moe", c, normed, NORMS["moe"] * TILES + CH * c + CH)
                if c is not first:
                    pe.wait_ge(logits_saved, c)
                for t in range(CH):
                    mm = nc.tensor.matmul(ps[:, 1, t * EXPERTS:(t + 1) * EXPERTS], stageT[:, t * P:(t + 1) * P], gate_sb[:], start=True, stop=True)
                mm.then_inc(logits_done, 1)

            gates(first)
            with pe.Fori(1, CHUNKS) as c:
                gates(c)
            pe.wait_ge(mask_done, 1)
            pe.wait_ge(setup_dve, 3)
            flat = mask_b[:].rearrange("p t e -> p (t e)")
            nc.tensor.matmul(ps[:, 2, 0:ER], triu_b[:], flat, start=True, stop=False, skip_group_check=True)
            for t in range(1, TILES):
                mm = nc.tensor.matmul(ps[:, 2, t * EXPERTS:ER], ones_b[:], flat[:, 0:ER - t * EXPERTS], start=False,
                                      stop=(t == TILES - 1), skip_group_check=True)
            mm.then_inc(cum_done, 1)

            def expert_rows(e):
                s = (e // XB) % 2
                pe.wait_ge(xg_in[s], 16 * (e // RING + 1))
                if e >= 2:
                    pe.wait_ge(xeT_done, e - 1)
                for a in range(2):
                    mm = nc.tensor.transpose(ps[:, e % 2, a * CAPH:(a + 1) * CAPH], xg[:, s, 2 * (e % XB) + a, :], ident[0:CAPH, 0:CAPH])
                mm.then_inc(xe_T, 1)

            def expert_up(e):
                r = e % RING
                pe.wait_ge(w_in[r] if e < RING else w_again[r], 32)
                pe.wait_ge(xeT_done, e + 1)
                if e >= 2:
                    pe.wait_ge(relu_done, 2 * (e - 2) + 2)
                for bank in range(2):
                    for i in range(2):
                        c = 2 * bank + i
                        mm = nc.tensor.matmul(ps[:, 2 + 2 * (e % 2) + bank, i * CAP:(i + 1) * CAP],
                                              w1_ring[:, r, c * P:(c + 1) * P], xeT[:, e % 2, :], start=True, stop=True)
                    mm.then_inc(eh_done, 1)

            def expert_down(e):
                pe.wait_ge(relu_done, 2 * e + 2)
                if e >= 2:
                    pe.wait_ge(y_saved, e - 1)
                for a in range(2):
                    for c in range(HC):
                        mm = nc.tensor.matmul(ps[0:CAPH, 6 + e % 2, a * DM:(a + 1) * DM], ehT[:, e % 2, c, a * CAPH:(a + 1) * CAPH],
                                              w2_ring[:, e % RING, c, :], start=(c == 0), stop=(c == HC - 1))
                mm.then_inc(ey_done, 1)

            pe.wait_ge(logits_saved, CHUNKS)
            pe.wait_ge(slots_ready, 2)
            for e in range(EXPERTS):
                expert_rows(e)
                expert_up(e)
                if e:
                    expert_down(e - 1)
            expert_down(EXPERTS - 1)

            pe.wait_ge(relu_done, 2 * EXPERTS)
            pe.wait_ge(y_saved, EXPERTS)
            pe.wait_ge(late_in, 16 * 6)
            qkv(1, first)
            with pe.Fori(1, CHUNKS) as c:
                qkv(1, c)
            pe.wait_ge(q_saved[1], CHUNKS)
            pe.wait_ge(k_saved[1], CHUNKS)
            pe.wait_ge(v_saved[1], TILES)
            attention(1)
            project(1, first)
            with pe.Fori(1, CHUNKS) as c:
                project(1, c)
            pe.wait_ge(res_done[1], CHUNKS)
            pe.wait_ge(ff_in, 16 * 4)

            def mlp(c):
                transpose_chunk("mlp", c, normed, NORMS["mlp"] * TILES + CH * c + CH)
                for i in range(HC):
                    if c is not first:
                        pe.wait_ge(h_saved_a if i < 2 else h_saved_v, 2 * c)
                    nc.tensor.matmul(ps[:, 2 + i, :], ffw1_sb[:, i * P:(i + 1) * P], stageT[:], start=True, stop=True).then_inc(h_done, 1)
                pe.wait_ge(h_saved_a, 2 * c + 2)
                pe.wait_ge(h_saved_v, 2 * c + 2)
                if c is not first:
                    pe.wait_ge(added, c)
                for t in range(CH):
                    for i in range(HC):
                        nc.tensor.matmul(ps_out[:, t * P:(t + 1) * P], hT[:, i, t * P:(t + 1) * P], ffw2_sb[:, i, :], start=(i == 0), stop=False)
                    mm = nc.tensor.matmul(ps_out[:, t * P:(t + 1) * P], ones_row[:], ffb2_row[:], start=False, stop=True)
                mm.then_inc(ff_done, 1)

            mlp(first)
            with pe.Fori(1, CHUNKS) as c:
                mlp(c)

        @block.vector
        def _(dve):
            first = 0

            def row_stats(n, c, ready=None, count=None):
                if ready is not None:
                    dve.wait_ge(ready, count)
                for t in range(CH):
                    last = nc.vector.bn_stats(stats[:, bass.ds(c * CH + t, 1), :].rearrange("p a s -> p (a s)"),
                                              x_sb[:, bass.ds(c * CH + t, 1), :].rearrange("p a s -> p (a s)"))
                last.then_inc(stats_done, 1)

            def finish_stats(n):
                k = 8 * n
                ev, od = stats[:, :, 1], stats[:, :, 4]
                dve.wait_ge(stats_done, CHUNKS * (n + 1))
                nc.vector.tensor_tensor(ln_t[:, 0, :], ev, od, ALU.add).then_inc(ln_step, 1)
                nc.vector.tensor_tensor(ln_t[:, 1, :], ev, od, ALU.subtract).then_inc(ln_step, 1)
                nc.vector.tensor_tensor(ln_t[:, 2, :], stats[:, :, 2], stats[:, :, 5], ALU.add).then_inc(ln_step, 1)
                dve.wait_ge(ln_step, k + 3)
                nc.vector.tensor_scalar(ln_mean[:], ln_t[:, 0, :], 0.5, None, ALU.mult).then_inc(ln_step, 1)
                nc.vector.tensor_tensor(ln_t[:, 3, :], ln_t[:, 1, :], ln_t[:, 1, :], ALU.mult).then_inc(ln_step, 1)
                nc.vector.tensor_scalar(ln_t[:, 4, :], ln_t[:, 2, :], 1.0 / DM, EPS, ALU.mult, ALU.add).then_inc(ln_step, 1)
                dve.wait_ge(ln_step, k + 6)
                nc.vector.tensor_scalar(ln_t[:, 3, :], ln_t[:, 3, :], 0.25, None, ALU.mult).then_inc(ln_step, 1)
                dve.wait_ge(ln_step, k + 7)
                nc.vector.tensor_tensor(ln_t[:, 5, :], ln_t[:, 4, :], ln_t[:, 3, :], ALU.add).then_inc(ln_step, 1)
                dve.wait_ge(rstd_done, n + 1)

            def normalize(use, c):
                if not (use == "qkv0" and c is first):
                    dve.wait_ge(stage_T, USE[use] * CHUNKS + c)
                if use == "moe" and c is not first:
                    dve.wait_ge(rows_kept, c)
                for t in range(CH):
                    nc.vector.tensor_scalar(stage[:, t, :], x_sb[:, bass.ds(c * CH + t, 1), :].rearrange("p a s -> p (a s)"),
                                            ln_mean[:, bass.ds(c * CH + t, 1)], ln_rstd[:, bass.ds(c * CH + t, 1)],
                                            ALU.subtract, ALU.mult).then_inc(normed, 1)

            def save_v(L, c, count):
                dve.wait_ge(proj_done[L], count)
                for t in range(CH):
                    dst = v_all[:, bass.ds(c * CH + t, 1)].rearrange("p a g (j d) -> p (a g) j d", d=HV)[:, :, :, 0:HD]
                    nc.vector.tensor_tensor(dst, ps_v[:, t * P:(t + 1) * P].rearrange("p (g j d) -> p g j d", g=GROUPS, j=JH),
                                            bv_b[L][:].rearrange("p (g j d) -> p g j d", g=GROUPS, j=JH), ALU.add).then_inc(v_saved[L], 1)

            def qkv0(c):
                normalize("qkv0", c)
                dve.wait_ge(proj_done[0], 3 * c + 2)
                nc.vector.tensor_scalar(qk_all[:, 1, bass.ds(c * CT, CT)], ps_k, bqk[0][:, 1:2], None, ALU.add).then_inc(k_saved[0], 1)
                save_v(0, c, 3 * c + 3)

            def qkv1(c):
                normalize("qkv1", c)
                for i, p in enumerate((ps_k, ps_kr)):
                    dve.wait_ge(proj_done[1], 5 * c + 3 + i)
                    nc.vector.tensor_scalar(rope_t[:, i, 1, :], p, bqk[1][:, 2 * i + 1:2 * i + 2], None, ALU.add).then_inc(rope_step, 1)
                dve.wait_ge(rope_q, 2 * c + 2)
                dve.wait_ge(rope_step, 6 * c + 2)
                for i, f in enumerate((cos_t, sin_t)):
                    nc.vector.tensor_tensor(rope_t[:, i], rope_t[:, i], f[:].unsqueeze(1).to_broadcast([P, 2, CT]), ALU.mult).then_inc(rope_step, 2)
                dve.wait_ge(rope_step, 6 * c + 6)
                nc.vector.tensor_tensor(qk_all[:, 0, bass.ds(c * CT, CT)], rope_t[:, 0, 0, :], rope_t[:, 1, 0, :], ALU.add).then_inc(q_saved[1], 1)
                nc.vector.tensor_tensor(qk_all[:, 1, bass.ds(c * CT, CT)], rope_t[:, 0, 1, :], rope_t[:, 1, 1, :], ALU.add).then_inc(k_saved[1], 1)
                save_v(1, c, 5 * c + 5)

            def top_half(it, hp):
                s = s_sb[:, hp]
                dve.wait_ge(scores_saved, 2 * it + hp + 1)
                dve.sem_inc(top_step, 1)
                k = 1
                for r in range(ROUNDS):
                    src = s if r == 0 else rest
                    for u in range(4):
                        if r:
                            dve.wait_ge(top_step, k - 3)
                        nc.vector.max(top[:, u, 8 * r:8 * r + 8], src[:, u, :]).then_inc(top_step, 1)
                        k += 1
                    if r == 0:
                        dve.wait_ge(top_step, k)
                        nc.vector.tensor_scalar(negm[:, hp, :], top[:, :, 0], -SCALE, None, ALU.mult).then_inc(neg_done[0], 1)
                    if r < ROUNDS - 1:
                        for u in range(4):
                            dve.wait_ge(top_step, k - 3)
                            nc.vector.match_replace(rest[:, u, :], top[:, u, 8 * r:8 * r + 8], src[:, u, :], NEG).then_inc(top_step, 1)
                            k += 1
                dve.wait_ge(top_step, k)
                dve.sem_clear(top_step)
                for u in range(4):
                    dve.wait_ge(exp_done[0], 4 * (2 * it + hp) + u + 1)
                    nc.vector.scalar_tensor_tensor(out=e_sb[:, hp, u, :], in0=s[:, u, :], scalar=top[:, u, TOPU - 1:TOPU],
                                                   in1=e_sb[:, hp, u, :], op0=ALU.is_ge, op1=ALU.mult).then_inc(probs_done, 1)

            def max_half(it, hp):
                s = ps_scores(hp)
                dve.wait_ge(scores_done[1], 2 * it + hp + 1)
                nc.vector.tensor_reduce(top[:, :, hp], s, AX_X, ALU.max).then_inc(max_done, 1)
                dve.wait_ge(max_done, 2 * it + hp + 1)
                nc.vector.tensor_scalar(negm[:, hp, :], top[:, :, hp], -SCALE, None, ALU.mult).then_inc(neg_done[1], 1)

            def contexts(L, it):
                b, g = it // GROUPS, it % GROUPS
                dve.wait_ge(ctx_T[L], it + 1)
                v = ps_ctx.rearrange("p (q j d) -> p q j d", q=KT, j=JH)
                nc.vector.reciprocal(recip[:], v[:, :, :, HD]).then_inc(recip_done[L], 1)
                dve.wait_ge(recip_done[L], it + 1)
                dst = xn_all[:, bass.ds(b * KT, KT), bass.ds(g * JH * HD, JH * HD)].rearrange("p q (j d) -> p q j d", d=HD)
                nc.vector.tensor_tensor(dst, v[:, :, :, 0:HD], recip[:].unsqueeze(3).to_broadcast([P, KT, JH, HD]), ALU.mult)\
                    .then_inc(ctx_done[L], 1)

            def attention(L):
                half = top_half if L == 0 else max_half
                for it in range(2):
                    half(it, 0)
                    half(it, 1)
                with dve.Fori(2, ITERS) as it:
                    half(it, 0)
                    contexts(L, it - 2)
                    half(it, 1)
                contexts(L, ITERS - 2)
                contexts(L, ITERS - 1)

            def project(L, c):
                n = 1 if L == 0 else 3
                if c is first:
                    dve.wait_ge(ctx_done[L], ITERS)
                dve.wait_ge(stage_T, USE[f"out{L}"] * CHUNKS + c)
                nc.vector.tensor_copy(stage[:], xn_all[:, bass.ds(c * CH, CH), :]).then_inc(ctx_staged[L], 1)
                dve.wait_ge(out_done[L], c + 1)
                xs = x_sb[:, bass.ds(c * CH, CH), :]
                nc.vector.tensor_tensor(xs, xs, ps_out.rearrange("p (t d) -> p t d", d=DM), ALU.add).then_inc(res_done[L], 1)
                row_stats(n, c, res_done[L], c + 1)

            nc.vector.memset(ones_b[:], 1.0).then_inc(setup_dve, 1)
            nc.vector.memset(zero_rows[:], 0.0).then_inc(setup_dve, 1)
            dve.wait_ge(x_in, 16)
            with dve.Fori(0, CHUNKS) as c:
                row_stats(0, c)
            finish_stats(0)
            dve.wait_ge(consts_in, 16 * 6)
            qkv0(first)
            with dve.Fori(1, CHUNKS) as c:
                qkv0(c)
            attention(0)
            project(0, first)
            with dve.Fori(1, CHUNKS) as c:
                project(0, c)
            finish_stats(1)
            dve.wait_ge(route_in, 16 * 4)
            nc.vector.tensor_copy(triu_b[:], triu[:]).then_inc(setup_dve, 1)
            normalize("moe", first)
            with dve.Fori(1, CHUNKS) as c:
                normalize("moe", c)

            steps = [0]

            def step(ins):
                ins.then_inc(rstep, 1)
                steps[0] += 1
                dve.wait_ge(rstep, steps[0])

            def col(a):
                return a.unsqueeze(2).to_broadcast([P, TILES, EXPERTS])

            lmax, who, esum, prob, place, keep, slot, tmp, weight = (rs[:, i, :] for i in range(9))
            dve.wait_ge(logits_saved, CHUNKS)
            step(nc.vector.tensor_reduce(lmax, logits[:], AX_X, ALU.max))
            step(nc.vector.tensor_tensor(rt[:, 0], logits[:], col(lmax), ALU.subtract))
            step(nc.vector.tensor_scalar(rt[:, 2], rt[:, 0], 0.0, None, ALU.is_ge))
            step(nc.vector.tensor_tensor(rt[:, 2], rt[:, 2], rev[:], ALU.mult))
            step(nc.vector.tensor_reduce(who, rt[:, 2], AX_X, ALU.max))
            step(nc.vector.tensor_tensor(rt[:, 3], rt[:, 2], col(who), ALU.is_equal))
            nc.vector.tensor_copy(mask_b[:], rt[:, 3]).then_inc(mask_done, 1)
            dve.wait_ge(gate_exp, 1)
            step(nc.vector.tensor_reduce(esum, rt[:, 1], AX_X, ALU.add))
            step(nc.vector.reciprocal(prob, esum))
            dve.wait_ge(cum_done, 1)
            step(nc.vector.tensor_tensor(rt[:, 0], rt[:, 3], ps[:, 2, 0:ER].rearrange("p (t e) -> p t e", e=EXPERTS), ALU.mult))
            step(nc.vector.tensor_reduce(place, rt[:, 0], AX_X, ALU.add))
            step(nc.vector.tensor_scalar(keep, place, float(CAP), None, ALU.is_le))
            step(nc.vector.tensor_scalar(tmp, who, -float(CAP), float(EXPERTS * CAP - 1), ALU.mult, ALU.add))
            step(nc.vector.tensor_tensor(slot, tmp, place, ALU.add))
            step(nc.vector.tensor_tensor(tmp, slot, spill[:], ALU.subtract))
            step(nc.vector.tensor_tensor(tmp, tmp, keep, ALU.mult))
            nc.vector.tensor_tensor(slot_idx[:], tmp, spill[:], ALU.add).then_inc(slots_ready, 1)
            nc.vector.tensor_tensor(back_idx[:], slot, keep, ALU.mult).then_inc(slots_ready, 1)
            step(nc.vector.tensor_tensor(weight, prob, keep, ALU.mult))

            for e in range(EXPERTS):
                for bank in range(2):
                    dve.wait_ge(eh_done, 2 * e + bank + 1)
                    if e >= 2:
                        dve.wait_ge(ey_done, e - 1)
                    nc.vector.tensor_scalar(ehT[:, e % 2, 2 * bank:2 * bank + 2, :].rearrange("p c n -> p (c n)"),
                                            ps[:, 2 + 2 * (e % 2) + bank, 0:2 * CAP], 0.0, None, ALU.max).then_inc(relu_done, 1)
            dve.wait_ge(gathered, 16 * TILES)

            def add_moe(c):
                for t in range(CH):
                    xs = x_sb[:, bass.ds(c * CH + t, 1), :].rearrange("p a d -> p (a d)")
                    nc.vector.scalar_tensor_tensor(out=xs, in0=xn_all[:, bass.ds(c * CH + t, 1), :].rearrange("p a d -> p (a d)"),
                                                   scalar=rs[:, 8, bass.ds(c * CH + t, 1)], in1=xs, op0=ALU.mult, op1=ALU.add)\
                        .then_inc(moe_added, 1)
                row_stats(2, c, moe_added, CH * c + CH)

            with dve.Fori(0, CHUNKS) as c:
                add_moe(c)
            finish_stats(2)
            dve.wait_ge(late_in, 16 * 6)
            qkv1(first)
            with dve.Fori(1, CHUNKS) as c:
                qkv1(c)
            attention(1)
            project(1, first)
            with dve.Fori(1, CHUNKS) as c:
                project(1, c)
            finish_stats(3)
            dve.wait_ge(ff_in, 16 * 4)

            def mlp(c):
                normalize("mlp", c)
                for i in range(2, HC):
                    dve.wait_ge(h_done, HC * c + i + 1)
                    nc.vector.tensor_scalar(hT[:, i, :], ps[:, 2 + i, :], ffb1_sb[:, i:i + 1], 0.0, ALU.add, ALU.max).then_inc(h_saved_v, 1)
                dve.wait_ge(ff_done, c + 1)
                xs = x_sb[:, bass.ds(c * CH, CH), :]
                nc.vector.tensor_tensor(xs, xs, ps_out.rearrange("p (t d) -> p t d", d=DM), ALU.add).then_inc(added, 1)

            with dve.Fori(0, CHUNKS) as c:
                mlp(c)


def kernel(**inputs):
    import numpy as np
    import concourse.bacc as bacc
    from concourse.bass_utils import run_bass_kernel_spmd

    a = {k: np.asarray(v) for k, v in inputs.items()}
    f32 = np.float32
    swap = np.arange(DM) ^ 1

    def columns(*rows):
        return np.ascontiguousarray(np.stack(rows, axis=1))

    d = np.arange(DM) % HD
    inv_freq = (f32(1.0) / f32(10000.0) ** (np.arange(0, HD, 2, dtype=f32) / f32(HD))).astype(f32)
    angle = (inv_freq[d % (HD // 2)][:, None] * np.tile(np.arange(SEQ, dtype=f32), CT // SEQ)[None, :]).astype(f32)
    sign = np.where(d % 2 == 0, f32(-1), f32(1))[:, None]
    token = np.arange(TILES, dtype=f32)[None, :] * P + np.arange(P, dtype=f32)[:, None]
    arrays = {
        "x": a["L0_attn_x"],
        "w0": columns(*(a[f"L0_attn_W{n}"].T for n in "qkvo")),
        "bqk0": columns(a["L0_attn_bq"], a["L0_attn_bk"]),
        "bv0": a["L0_attn_bv"],
        "bo0": a["L0_attn_bo"][None, :],
        "gate": a["L0_ffn_gate_w"].T,
        "w1": a["L0_ffn_w1"],
        "w2": a["L0_ffn_w2"],
        "w5": columns(*(a[f"L1_attn_W{n}"].T for n in "qkvo"), a["L1_attn_Wq"][swap].T, a["L1_attn_Wk"][swap].T),
        "bqk1": columns(a["L1_attn_bq"], a["L1_attn_bk"], a["L1_attn_bq"][swap], a["L1_attn_bk"][swap]),
        "bv1": a["L1_attn_bv"],
        "bo1": a["L1_attn_bo"][None, :],
        "ffw1": a["L1_ffn_W1"],
        "ffb1": a["L1_ffn_b1"].reshape(HC, P).T,
        "ffw2": a["L1_ffn_W2"],
        "ffb2": a["L1_ffn_b2"][None, :],
        "ident_d": np.eye(P, dtype=f32),
        "hmask_d": (np.arange(DM)[:, None] // HD == np.arange(HEADS)[None, :]).astype(f32),
        "cos_d": np.cos(angle).astype(f32),
        "sin_d": (sign * np.sin(angle)).astype(f32),
        "triu_d": np.triu(np.ones((P, P), dtype=f32)),
        "rev_d": np.broadcast_to(EXPERTS - np.arange(EXPERTS, dtype=f32), (P, TILES, EXPERTS)),
        "spill_d": token + f32(SLOTS),
    }
    arrays = {k: np.ascontiguousarray(v) for k, v in arrays.items()}
    nc = bacc.Bacc("TRN2", target_bir_lowering=False, num_devices=1)
    args = {k: nc.dram_tensor(f"in_{k}", v.shape, F32, kind="ExternalInput").ap() for k, v in arrays.items()}
    out = nc.dram_tensor("out_0", (BATCH, SEQ, DM), F32, kind="ExternalOutput").ap()
    build(nc, out=out, **args)
    r = run_bass_kernel_spmd(nc, [{f"in_{k}": v for k, v in arrays.items()}], core_ids=[0])
    return r.results[0]["out_0"]
```

```python
from contextlib import ExitStack

import concourse.bass as bass
from concourse import mybir

F32 = mybir.dt.float32
BF16 = mybir.dt.bfloat16
U32 = mybir.dt.uint32
ALU = mybir.AluOpType
ACT = mybir.ActivationFunctionType
AX_X = mybir.AxisListType.X

P = 128
BATCH, SEQ, DM = 8, 256, 128
HEADS = 16
HD = DM // HEADS
HV = HD + 1
TILES = BATCH * SEQ // P
TOKENS = TILES * P
CH = 4
CHUNKS = TILES // CH
CT = CH * P
KT = SEQ // P
GROUPS = 4
JH = HEADS // GROUPS
ITERS = BATCH * GROUPS
VW = JH * HV
TOPU = 27
ROUNDS = 4
SCALE = HD ** -0.5
EPS = 1e-5
NEG = -3.0e38
EXPERTS, HID = 16, 512
HC = HID // P
CAP = 160
CAPH = CAP // 2
SLOTS = EXPERTS * CAP
RING = 8
XB = 4
ER = TILES * EXPERTS


def build(nc, x, w0, bqk0, bv0, bo0, gate, w1, w2, w5, bqk1, bv1, bo1, ffw1, ffb1, ffw2, ffb2,
          ident_d, hmask_d, cos_d, sin_d, triu_d, rev_d, spill_d, out):
    with ExitStack() as ctx:
        def sb(name, shape, dt=F32):
            return ctx.enter_context(nc.sbuf_tensor(name, shape, dt))

        def sem(name):
            return ctx.enter_context(nc.semaphore(name))

        def pair(name):
            return [sem(f"{name}0"), sem(f"{name}1")]

        dispatched = nc.dram_tensor("dispatched", (SLOTS + TOKENS, DM), F32, kind="Internal").ap()
        expert_out = nc.dram_tensor("expert_out", (SLOTS, DM), F32, kind="Internal").ap()

        ident = sb("ident", [P, P])
        neg_half = sb("neg_half", [P, TILES])
        hmask = sb("hmask", [P, HEADS])
        wqkvo = [sb("wqkvo0", [P, 4, DM]), sb("wqkvo1", [P, 6, DM])]
        bqk = [sb("bqk0_sb", [P, 2]), sb("bqk1_sb", [P, 4])]
        bv_b = [sb("bv0_sb", [P, DM]), sb("bv1_sb", [P, DM])]
        bo_b = [sb("bo0_sb", [P, DM]), sb("bo1_sb", [P, DM])]
        cos_t = sb("cos_t", [P, CT])
        sin_t = sb("sin_t", [P, CT])
        gate_sb = sb("gate_sb", [P, EXPERTS])
        triu = sb("triu", [P, P])
        zero_rows = sb("zero_rows", [P, DM])
        triu_b = sb("triu_b", [P, P], BF16)
        ones_b = sb("ones_b", [P, P], BF16)
        rev = sb("rev", [P, TILES, EXPERTS])
        spill = sb("spill", [P, TILES])
        ffw1_sb = sb("ffw1_sb", [P, HID])
        ffw2_sb = sb("ffw2_sb", [P, HC, DM])
        ffb1_sb = sb("ffb1_sb", [P, HC])
        ffb2_b = sb("ffb2_b", [P, DM])
        w1_ring = sb("w1_ring", [P, RING, HID])
        w2_ring = sb("w2_ring", [P, RING, HC, DM])
        x_sb = sb("x_sb", [P, TILES, DM])
        xn_all = sb("xn_all", [P, TILES, DM])
        stats = sb("stats", [P, TILES, 6])
        ln_mv = sb("ln_mv", [P, TILES, 2])
        ln_ve = sb("ln_ve", [P, TILES])
        ln_rstd = sb("ln_rstd", [P, TILES])
        rowsT = sb("rowsT", [P, 2, CT])
        rope_t = sb("rope_t", [P, 2, 2, CT])
        qk_all = sb("qk_all", [P, 2, TOKENS])
        q_st = sb("q_st", [P, JH, SEQ])
        v_all = sb("v_all", [P, TILES, GROUPS, VW])
        v_st = sb("v_st", [P, KT, JH, 32])
        ot_sb = sb("ot_sb", [P, SEQ])
        top = sb("top", [P, 4, 8 * ROUNDS])
        rest = sb("rest", [P, 4, SEQ])
        negm = sb("negm", [P, 2, 4])
        s_sb = sb("s_sb", [P, 2, 4, SEQ])
        e_sb = sb("e_sb", [P, 2, 4, SEQ])
        pt_sb = sb("pt_sb", [P, 2, 2, KT, SEQ])
        recip = sb("recip", [P, KT, JH])
        hT = sb("hT", [P, 2, HC, CT])
        logits = sb("logits", [P, TILES, EXPERTS])
        rt = sb("rt", [P, 4, TILES, EXPERTS])
        mask_b = sb("mask_b", [P, TILES, EXPERTS], BF16)
        rs = sb("rs", [P, 12, TILES])
        slot_idx = sb("slot_idx", [P, TILES], U32)
        back_idx = sb("back_idx", [P, TILES], U32)
        xg = sb("xg", [CAPH, 2, XB * 2, DM])
        y_sb = sb("y_sb", [CAPH, RING, 2, DM])
        ehT = sb("ehT", [P, 2, HC, CAP])
        xeT = sb("xeT", [P, 2, CAP])

        ps = ctx.enter_context(nc.psum_tensor("ps", [P, 8, 512], F32))

        x_in = [sem(f"x_in{c}") for c in range(CHUNKS)]
        consts_in, late_in, route_in, ff_in = sem("consts_in"), sem("late_in"), sem("route_in"), sem("ff_in")
        setup_done = sem("setup_done")
        setup_dve = sem("setup_dve")
        stats_done = sem("stats_done")
        ln_step = sem("ln_step")
        rstd_done = sem("rstd_done")
        normed = sem("normed")
        bias_added = sem("bias_added")
        rows_T = sem("rows_T")
        rowsT_saved = sem("rowsT_saved")
        proj_done = pair("proj_done")
        q_saved, k_saved, v_saved = pair("q_saved"), pair("k_saved"), pair("v_saved")
        rope_step, rope_q = sem("rope_step"), sem("rope_q")
        q_staged, v_staged = pair("q_staged"), pair("v_staged")
        scores_done = pair("scores_done")
        top_step = sem("top_step")
        max_done = sem("max_done")
        neg_done = pair("neg_done")
        exp_done = pair("exp_done")
        scores_saved = sem("scores_saved")
        probs_done = sem("probs_done")
        probs_T = pair("probs_T")
        pt_done = pair("pt_done")
        pv_done = pair("pv_done")
        ot_saved = pair("ot_saved")
        ctx_T = pair("ctx_T")
        recip_done, ctx_done = pair("recip_done"), pair("ctx_done")
        out_done, res_done = pair("out_done"), pair("res_done")
        logits_done, logits_saved = sem("logits_done"), sem("logits_saved")
        rstep = sem("rstep")
        gate_exp = sem("gate_exp")
        mask_done = sem("mask_done")
        cum_done = sem("cum_done")
        slots_ready = sem("slots_ready")
        zeroed = sem("zeroed")
        scattered = sem("scattered")
        xg_in = [sem(f"xg_in{s}") for s in range(2)]
        w_in = [sem(f"w_in{r}") for r in range(RING)]
        w_again = [sem(f"w_again{r}") for r in range(RING)]
        xe_T, xeT_done = sem("xe_T"), sem("xeT_done")
        eh_done, relu_done = sem("eh_done"), sem("relu_done")
        ey_done, y_saved = sem("ey_done"), sem("y_saved")
        y_out = sem("y_out")
        gathered = [sem(f"gathered{c}") for c in range(CHUNKS)]
        moe_added = sem("moe_added")
        h_done, h_saved_a, h_saved_v = sem("h_done"), sem("h_saved_a"), sem("h_saved_v")
        ff_done, added = sem("ff_done"), sem("added")
        stored = sem("stored")

        block = ctx.enter_context(nc.Block())

        ps_q, ps_k, ps_v, ps_qr, ps_kr = (ps[:, i, :] for i in range(2, 7))

        def ps_T(m):
            return ps[:, m % 2, :]

        ps_out, ps_down = ps[:, 2, :], ps[:, 3, :]

        def ps_logits(c):
            return ps[:, 4 + c % 2, 0:CH * EXPERTS]

        def ps_scores(hp):
            return ps[:, 2 * hp:2 * hp + 2, :].rearrange("p a (b n) -> p (a b) n", b=KT)

        ps_o = ps[:, 6, 0:SEQ]
        ps_ctx = ps[:, 7, 0:SEQ]

        def staggered(a, b):
            order = [(a, 0), (a, 1)] + [e for c in range(2, CHUNKS) for e in ((a, c), (b, c - 2))]
            return order + [(b, CHUNKS - 2), (b, CHUNKS - 1)]

        IN0 = [("qkv0", c) for c in range(CHUNKS)]
        OUT0 = staggered("out0", "gates")
        IN1 = [("qkv1", c) for c in range(CHUNKS)]
        OUT1 = staggered("out1", "mlp")
        AT = {e: m for m, e in enumerate(IN0 + OUT0 + IN1 + OUT1)}
        NORMS = {"qkv0": 0, "gates": 1, "qkv1": 2, "mlp": 3}

        @block.sync
        def _(sp):
            rows = x.rearrange("b (t p) d -> p (b t) d", p=P)
            for c in range(CHUNKS):
                sp.dma_start(x_sb[:, c * CH:(c + 1) * CH, :], rows[:, c * CH:(c + 1) * CH, :]).then_inc(x_in[c], 16)
            for dst, src in ((ident[:], ident_d), (hmask[:], hmask_d), (wqkvo[0][:], w0), (bqk[0][:], bqk0),
                             (bv_b[0][:], bv0.partition_broadcast(P)), (bo_b[0][:], bo0.partition_broadcast(P))):
                sp.dma_start(dst, src).then_inc(consts_in, 16)
            for dst, src in ((wqkvo[1][:], w5), (bqk[1][:], bqk1), (bv_b[1][:], bv1.partition_broadcast(P)),
                             (bo_b[1][:], bo1.partition_broadcast(P)), (cos_t[:], cos_d), (sin_t[:], sin_d)):
                sp.dma_start(dst, src).then_inc(late_in, 16)
            for dst, src in ((gate_sb[:], gate), (triu[:], triu_d), (rev[:], rev_d), (spill[:], spill_d)):
                sp.dma_start(dst, src).then_inc(route_in, 16)
            for dst, src in ((ffw1_sb[:], ffw1), (ffw2_sb[:], ffw2.rearrange("(c p) d -> p c d", p=P)),
                             (ffb1_sb[:], ffb1), (ffb2_b[:], ffb2.partition_broadcast(P))):
                sp.dma_start(dst, src).then_inc(ff_in, 16)
            for r in range(RING):
                sp.dma_start(w1_ring[:, r, :], w1[r]).then_inc(w_in[r], 16)
                sp.dma_start(w2_ring[:, r], w2[r].rearrange("(c p) d -> p c d", p=P)).then_inc(w_in[r], 16)
            sp.wait_ge(setup_dve, 2)
            sp.dma_start(dispatched[0:SLOTS, :].rearrange("(a p) d -> p a d", p=P), zero_rows[:].unsqueeze(1).to_broadcast([P, SLOTS // P, DM])).then_inc(zeroed, 16)
            sp.wait_ge(scattered, 16 * TILES)

            def load_rows(i, s):
                e0 = i * RING + s * XB
                sp.dma_start(xg[:, s], dispatched[bass.ds(e0 * CAP, XB * CAP), :].rearrange("(a p) d -> p a d", p=CAPH))\
                    .then_inc(xg_in[s], 16)

            def store_rows(i, r):
                e = i * RING + r
                sp.wait_ge(y_saved, i * RING + r + 1)
                sp.dma_start(expert_out[bass.ds(e * CAP, CAP), :].rearrange("(a p) d -> p a d", p=CAPH), y_sb[:, r])\
                    .then_inc(y_out, 16)

            load_rows(0, 0)
            load_rows(0, 1)
            for r in range(RING):
                store_rows(0, r)
                if r % XB == XB - 1:
                    load_rows(1, r // XB)
            for r in range(RING):
                store_rows(1, r)
            with sp.Fori(0, CHUNKS) as c:
                sp.wait_ge(added, c + 1)
                sp.dma_start(out.rearrange("b (t p) d -> p (b t) d", p=P)[:, bass.ds(c * CH, CH), :],
                             x_sb[:, bass.ds(c * CH, CH), :]).then_inc(stored, 16)
            sp.wait_ge(stored, 16 * CHUNKS)

        @block.gpsimd
        def _(pool):
            nc.gpsimd.memset(neg_half[:], -0.5).then_inc(setup_done, 1)
            nc.gpsimd.memset(v_st[:], 0.0).then_inc(setup_done, 1)
            nc.gpsimd.memset(v_all[:], 1.0).then_inc(setup_done, 1)

            def rstd(n, c):
                pool.wait_ge(ln_step, (CH + 1) * (n * CHUNKS + c + 1))
                if n == 0 and c == 0:
                    pool.wait_ge(setup_done, 1)
                cs = slice(c * CH, (c + 1) * CH)
                nc.gpsimd.tensor_tensor(ln_rstd[:, cs], ln_ve[:, cs], neg_half[:, cs], ALU.pow).then_inc(rstd_done, 1)

            def add_bias(n, c, bias):
                pool.wait_ge(normed, CH * (n * CHUNKS + c + 1))
                xs = x_sb[:, c * CH:(c + 1) * CH, :]
                nc.gpsimd.tensor_tensor(xs, xs, bias[:].unsqueeze(1).to_broadcast([P, CH, DM]), ALU.add).then_inc(bias_added, 1)

            def stage_q(L, it, hp):
                b, g = it // GROUPS, it % GROUPS
                if it is not first:
                    pool.wait_ge(scores_done[L], 2 * it + hp - 1)
                q = qk_all[:, 0, bass.ds(b * SEQ, SEQ)].unsqueeze(1).to_broadcast([P, 2, SEQ])
                m = hmask[:, bass.ds(g * JH + 2 * hp, 2)].unsqueeze(2).to_broadcast([P, 2, SEQ])
                nc.gpsimd.tensor_tensor(q_st[:, 2 * hp:2 * hp + 2, :], q, m, ALU.mult).then_inc(q_staged[L], 1)

            def stage_v(L, it):
                b, g = it // GROUPS, it % GROUPS
                if it is not first:
                    pool.wait_ge(pv_done[L], 2 * it)
                nc.gpsimd.tensor_copy(
                    v_st[:, :, :, 0:HV],
                    v_all[:, bass.ds(b * KT, KT), bass.ds(g, 1), :].rearrange("p t a (j d) -> p t (a j) d", d=HV),
                ).then_inc(v_staged[L], 1)

            first = 0

            def stage_all(L):
                pool.wait_ge(q_saved[L], CHUNKS)
                pool.wait_ge(v_saved[L], TILES)
                if L == 0:
                    pool.wait_ge(setup_done, 3)
                    pool.wait_ge(consts_in, 16 * 6)
                for it in range(2):
                    stage_q(L, it, 0)
                    stage_q(L, it, 1)
                stage_v(L, first)
                with pool.Fori(2, ITERS) as it:
                    stage_q(L, it, 0)
                    stage_q(L, it, 1)
                    stage_v(L, it - 1)
                stage_v(L, ITERS - 1)

            for c in range(CHUNKS):
                rstd(0, c)
            pool.wait_ge(consts_in, 16 * 6)
            for c in range(CHUNKS):
                add_bias(0, c, bo_b[0])
            stage_all(0)
            for c in range(CHUNKS):
                rstd(1, c)
            pool.wait_ge(zeroed, 16)
            pool.wait_ge(slots_ready, 2)
            for t in range(TILES):
                pool.indirect_dma_start(dispatched[:, :], bass.IndirectOffsetOnAxis(slot_idx[:, t:t + 1], 0),
                                        xn_all[:, t, :], None).then_inc(scattered, 16)
            for r in range(RING):
                pool.wait_ge(ey_done, r + 1)
                pool.dma_start(w1_ring[:, r, :], w1[RING + r]).then_inc(w_again[r], 16)
                pool.dma_start(w2_ring[:, r], w2[RING + r].rearrange("(c p) d -> p c d", p=P)).then_inc(w_again[r], 16)
            pool.wait_ge(y_out, 16 * EXPERTS)
            pool.wait_ge(scattered, 16 * TILES)
            for t in range(TILES):
                pool.indirect_dma_start(xn_all[:, t, :], None, expert_out[:, :],
                                        bass.IndirectOffsetOnAxis(back_idx[:, t:t + 1], 0)).then_inc(gathered[t // CH], 16)
            for c in range(CHUNKS):
                rstd(2, c)
            pool.wait_ge(late_in, 16 * 6)
            for c in range(CHUNKS):
                add_bias(2, c, bo_b[1])
            stage_all(1)
            pool.wait_ge(ff_in, 16 * 4)
            for c in range(CHUNKS):
                rstd(3, c)
                if c:
                    add_bias(3, c - 1, ffb2_b)
            add_bias(3, CHUNKS - 1, ffb2_b)

        @block.scalar
        def _(act):
            def save_rowsT(use, c):
                m = AT[use, c]
                act.wait_ge(rows_T, m + 1)
                nc.scalar.activation(rowsT[:, m % 2, :], ps_T(m), ACT.Copy).then_inc(rowsT_saved, 1)

            def save_q(c):
                act.wait_ge(proj_done[0], 3 * c + 1)
                nc.scalar.activation(qk_all[:, 0, c * CT:(c + 1) * CT], ps_q, ACT.Identity, bias=bqk[0][:, 0:1]).then_inc(q_saved[0], 1)

            def save_rope_q(c):
                if c:
                    act.wait_ge(q_saved[1], c)
                for i, p in enumerate((ps_q, ps_qr)):
                    act.wait_ge(proj_done[1], 5 * c + 1 + i)
                    nc.scalar.activation(rope_t[:, i, 0, :], p, ACT.Identity, bias=bqk[1][:, 2 * i:2 * i + 1]).then_inc(rope_q, 1)

            def save_logits(c):
                act.wait_ge(logits_done, c + 1)
                nc.scalar.activation(logits[:, c * CH:(c + 1) * CH, :], ps_logits(c).rearrange("p (t e) -> p t e", e=EXPERTS),
                                     ACT.Copy).then_inc(logits_saved, 1)

            def save_hidden(c):
                for i in range(2):
                    act.wait_ge(h_done, HC * c + i + 1)
                    nc.scalar.activation(hT[:, c % 2, i, :], ps[:, 4 + i, :], ACT.Relu, bias=ffb1_sb[:, i:i + 1]).then_inc(h_saved_a, 1)

            after = {"qkv0": save_q, "gates": save_logits, "qkv1": save_rope_q, "mlp": save_hidden}

            def walk(entries):
                save_rowsT(*entries[0])
                for e, following in zip(entries, entries[1:] + [None]):
                    if following:
                        save_rowsT(*following)
                    if e[0] in after:
                        after[e[0]](e[1])

            def exps(L, it, hp):
                n = 2 * it + hp
                act.wait_ge(neg_done[L], n + 1)
                if it is not first:
                    act.wait_ge(probs_T[L], 2 * (2 * it + hp - 2) + 2)
                src = s_sb[:, hp] if L == 0 else ps_scores(hp)
                for u in range(4):
                    nc.scalar.activation(e_sb[:, hp, u, :], src[:, u, :], ACT.Exp,
                                         bias=negm[:, hp, u:u + 1], scale=SCALE).then_inc(exp_done[L], 1)

            def save_scores(it, hp):
                act.wait_ge(scores_done[0], 2 * it + hp + 1)
                if it is not first:
                    act.wait_ge(probs_done, 4 * (2 * it + hp - 1))
                nc.scalar.activation(s_sb[:, hp], ps_scores(hp), ACT.Copy).then_inc(scores_saved, 1)

            def save_pt(L, it, hp, jj):
                act.wait_ge(probs_T[L], 2 * (2 * it + hp) + jj + 1)
                if it is not first:
                    act.wait_ge(pv_done[L], 2 * it + hp - 1)
                nc.scalar.activation(pt_sb[:, hp, jj].rearrange("p a n -> p (a n)"), ps[:, 4 + jj, :], ACT.Copy).then_inc(pt_done[L], 1)

            def save_ot(L, it):
                act.wait_ge(pv_done[L], 2 * it + 2)
                if it is not first:
                    act.wait_ge(ctx_T[L], it)
                nc.scalar.activation(ot_sb[:], ps_o, ACT.Copy).then_inc(ot_saved[L], 1)

            first = 0

            def attention(L):
                def step(it, prev, last=False):
                    exps(L, it, 0)
                    if L == 0:
                        save_scores(it, 1)
                    if prev is not None:
                        save_pt(L, prev, 1, 0)
                        save_pt(L, prev, 1, 1)
                    exps(L, it, 1)
                    if L == 0 and not last:
                        save_scores(it + 1, 0)
                    save_pt(L, it, 0, 0)
                    save_pt(L, it, 0, 1)
                    if prev is not None:
                        save_ot(L, prev)

                if L == 0:
                    save_scores(first, 0)
                step(first, None)
                step(1, first)
                with act.Fori(2, ITERS - 1) as it:
                    step(it, it - 1)
                step(ITERS - 1, ITERS - 2, last=True)
                save_pt(L, ITERS - 1, 1, 0)
                save_pt(L, ITERS - 1, 1, 1)
                save_ot(L, ITERS - 1)

            act.wait_ge(consts_in, 16 * 6)
            walk(IN0)
            attention(0)
            walk(OUT0)
            act.wait_ge(rstep, 2)
            nc.scalar.activation(rt[:, 1], rt[:, 0], ACT.Exp).then_inc(gate_exp, 1)

            def save_y(e):
                act.wait_ge(ey_done, e + 1)
                if e >= RING:
                    act.wait_ge(y_out, 16 * (e - RING + 1))
                nc.scalar.activation(y_sb[:, e % RING].rearrange("p a d -> p (a d)"),
                                     ps[0:CAPH, 6 + e % 2, 0:2 * DM], ACT.Copy).then_inc(y_saved, 1)

            for e in range(EXPERTS):
                act.wait_ge(xe_T, e + 1)
                if e >= 2:
                    act.wait_ge(eh_done, 2 * (e - 2) + 2)
                nc.scalar.activation(xeT[:, e % 2, :], ps[:, e % 2, 0:CAP], ACT.Copy).then_inc(xeT_done, 1)
                if e >= 2:
                    save_y(e - 2)
            save_y(EXPERTS - 2)
            save_y(EXPERTS - 1)
            act.wait_ge(late_in, 16 * 6)
            walk(IN1)
            attention(1)
            act.wait_ge(ff_in, 16 * 4)
            walk(OUT1)

        @block.tensor
        def _(pe):
            first = 0

            def turn_rows(use, c):
                m = AT[use, c]
                if use in NORMS:
                    pe.wait_ge(normed, CH * (NORMS[use] * CHUNKS + c + 1))
                if m >= 2:
                    pe.wait_ge(rowsT_saved, m - 1)
                for t in range(CH):
                    mm = nc.tensor.transpose(ps_T(m)[:, t * P:(t + 1) * P], xn_all[:, c * CH + t, :], ident[:])
                mm.then_inc(rows_T, 1)

            def qkv(L, c, rT, tile):
                w = wqkvo[L]
                if c:
                    pe.wait_ge(q_saved[L], c)
                    pe.wait_ge(k_saved[L], c)
                    pe.wait_ge(v_saved[L], CH * c)
                nc.tensor.matmul(ps_q, w[:, 0, :], rT, start=True, stop=True).then_inc(proj_done[L], 1)
                if L == 1:
                    nc.tensor.matmul(ps_qr, w[:, 4, :], rT, start=True, stop=True).then_inc(proj_done[L], 1)
                nc.tensor.matmul(ps_k, w[:, 1, :], rT, start=True, stop=True).then_inc(proj_done[L], 1)
                if L == 1:
                    nc.tensor.matmul(ps_kr, w[:, 5, :], rT, start=True, stop=True).then_inc(proj_done[L], 1)
                for t in range(CH):
                    mm = nc.tensor.matmul(ps_v[:, t * P:(t + 1) * P], tile(t), w[:, 2, :], start=True, stop=True)
                mm.then_inc(proj_done[L], 1)

            def project(L, c, tile):
                if c:
                    pe.wait_ge(res_done[L], c)
                for t in range(CH):
                    mm = nc.tensor.matmul(ps_out[:, t * P:(t + 1) * P], tile(t), wqkvo[L][:, 3, :], start=True, stop=True)
                mm.then_inc(out_done[L], 1)

            def gates(c, tile):
                if c >= 2:
                    pe.wait_ge(logits_saved, c - 1)
                for t in range(CH):
                    mm = nc.tensor.matmul(ps_logits(c)[:, t * EXPERTS:(t + 1) * EXPERTS], tile(t), gate_sb[:], start=True, stop=True)
                mm.then_inc(logits_done, 1)

            def mlp(c, rT):
                for i in range(HC):
                    if c:
                        pe.wait_ge(h_saved_a if i < 2 else h_saved_v, 2 * c)
                    nc.tensor.matmul(ps[:, 4 + i, :], ffw1_sb[:, i * P:(i + 1) * P], rT, start=True, stop=True).then_inc(h_done, 1)
                if c:
                    mlp_down(c - 1)
                if c == CHUNKS - 1:
                    mlp_down(c)

            def mlp_down(c):
                pe.wait_ge(h_saved_a, 2 * c + 2)
                pe.wait_ge(h_saved_v, 2 * c + 2)
                if c:
                    pe.wait_ge(added, c)
                for t in range(CH):
                    for i in range(HC):
                        mm = nc.tensor.matmul(ps_down[:, t * P:(t + 1) * P], hT[:, c % 2, i, t * P:(t + 1) * P], ffw2_sb[:, i, :],
                                              start=(i == 0), stop=(i == HC - 1))
                mm.then_inc(ff_done, 1)

            def product(use, c):
                m = AT[use, c]
                pe.wait_ge(rowsT_saved, m + 1)
                rT = rowsT[:, m % 2, :]

                def tile(t):
                    return rT[:, t * P:(t + 1) * P]

                if use in ("qkv0", "qkv1"):
                    qkv(int(use[3]), c, rT, tile)
                elif use in ("out0", "out1"):
                    project(int(use[3]), c, tile)
                elif use == "gates":
                    gates(c, tile)
                else:
                    mlp(c, rT)

            def walk(entries):
                turn_rows(*entries[0])
                for e, following in zip(entries, entries[1:] + [None]):
                    if following:
                        turn_rows(*following)
                    product(*e)

            weights_ready = [probs_done, exp_done[1]]
            scores_read, per_half = [scores_saved, exp_done[1]], [1, 4]

            def scores(L, it, hp):
                if True:
                    pe.wait_ge(q_staged[L], 2 * it + hp + 1)
                if it is not first:
                    pe.wait_ge(scores_read[L], per_half[L] * (2 * it + hp - 1))
                b = it // GROUPS
                for jj in range(2):
                    for qt in range(KT):
                        mm = nc.tensor.matmul(ps_scores(hp)[:, 2 * jj + qt, :], q_st[:, 2 * hp + jj, qt * P:(qt + 1) * P],
                                              qk_all[:, 1, bass.ds(b * SEQ, SEQ)], start=True, stop=True)
                mm.then_inc(scores_done[L], 1)

            def turn(L, it, hp):
                n = 2 * it + hp
                for jj in range(2):
                    pe.wait_ge(weights_ready[L], 4 * n + 2 * jj + 2)
                    if not (it is first and hp == 0):
                        pe.wait_ge(pt_done[L], 2 * n + jj - 1)
                    for kt in range(KT):
                        for qt in range(KT):
                            mm = nc.tensor.transpose(ps[:, 4 + jj, kt * SEQ + qt * P:kt * SEQ + (qt + 1) * P],
                                                     e_sb[:, hp, 2 * jj + qt, kt * P:(kt + 1) * P], ident[:])
                    mm.then_inc(probs_T[L], 1)

            def sum_values(L, it, hp):
                n = 2 * it + hp
                if hp == 0:
                    pe.wait_ge(v_staged[L], it + 1)
                    if it is not first:
                        pe.wait_ge(ot_saved[L], it)
                pe.wait_ge(pt_done[L], 2 * n + 2)
                for kt in range(KT):
                    for jj in range(2):
                        j = 2 * hp + jj
                        mm = nc.tensor.matmul(ps_o[32 * j:32 * j + 32, :], v_st[:, kt, j, :], pt_sb[:, hp, jj, kt, :],
                                              start=(kt == 0), stop=(kt == KT - 1), skip_group_check=True)
                mm.then_inc(pv_done[L], 1)

            def turn_back(L, it):
                pe.wait_ge(ot_saved[L], it + 1)
                if it is not first:
                    pe.wait_ge(ctx_done[L], it)
                for qt in range(KT):
                    mm = nc.tensor.transpose(ps_ctx[:, qt * P:(qt + 1) * P], ot_sb[:, qt * P:(qt + 1) * P], ident[:])
                mm.then_inc(ctx_T[L], 1)

            def attention(L):
                scores(L, first, 0)
                scores(L, first, 1)
                turn(L, first, 0)
                scores(L, 1, 0)
                turn(L, first, 1)
                sum_values(L, first, 0)
                scores(L, 1, 1)
                turn(L, 1, 0)
                sum_values(L, first, 1)
                with pe.Fori(2, ITERS) as it:
                    scores(L, it, 0)
                    turn(L, it - 1, 1)
                    turn_back(L, it - 2)
                    sum_values(L, it - 1, 0)
                    scores(L, it, 1)
                    turn(L, it, 0)
                    sum_values(L, it - 1, 1)
                turn(L, ITERS - 1, 1)
                turn_back(L, ITERS - 2)
                sum_values(L, ITERS - 1, 0)
                sum_values(L, ITERS - 1, 1)
                turn_back(L, ITERS - 1)

            pe.wait_ge(consts_in, 16 * 6)
            walk(IN0)
            pe.wait_ge(q_saved[0], CHUNKS)
            pe.wait_ge(k_saved[0], CHUNKS)
            pe.wait_ge(v_saved[0], TILES)
            attention(0)
            pe.wait_ge(route_in, 16 * 4)
            pe.wait_ge(ctx_done[0], ITERS)
            walk(OUT0)
            pe.wait_ge(mask_done, 1)
            pe.wait_ge(setup_dve, 3)
            flat = mask_b[:].rearrange("p t e -> p (t e)")
            nc.tensor.matmul(ps[:, 6, 0:ER], triu_b[:], flat, start=True, stop=False, skip_group_check=True)
            for t in range(1, TILES):
                mm = nc.tensor.matmul(ps[:, 6, t * EXPERTS:ER], ones_b[:], flat[:, 0:ER - t * EXPERTS], start=False,
                                      stop=(t == TILES - 1), skip_group_check=True)
            mm.then_inc(cum_done, 1)

            def expert_rows(e):
                s = (e // XB) % 2
                pe.wait_ge(xg_in[s], 16 * (e // RING + 1))
                if e >= 2:
                    pe.wait_ge(xeT_done, e - 1)
                for a in range(2):
                    mm = nc.tensor.transpose(ps[:, e % 2, a * CAPH:(a + 1) * CAPH], xg[:, s, 2 * (e % XB) + a, :], ident[0:CAPH, 0:CAPH])
                mm.then_inc(xe_T, 1)

            def expert_up(e):
                r = e % RING
                pe.wait_ge(w_in[r] if e < RING else w_again[r], 32)
                pe.wait_ge(xeT_done, e + 1)
                if e >= 2:
                    pe.wait_ge(relu_done, 2 * (e - 2) + 2)
                for bank in range(2):
                    for i in range(2):
                        c = 2 * bank + i
                        mm = nc.tensor.matmul(ps[:, 2 + 2 * (e % 2) + bank, i * CAP:(i + 1) * CAP],
                                              w1_ring[:, r, c * P:(c + 1) * P], xeT[:, e % 2, :], start=True, stop=True)
                    mm.then_inc(eh_done, 1)

            def expert_down(e):
                pe.wait_ge(relu_done, 2 * e + 2)
                if e >= 2:
                    pe.wait_ge(y_saved, e - 1)
                for a in range(2):
                    for c in range(HC):
                        mm = nc.tensor.matmul(ps[0:CAPH, 6 + e % 2, a * DM:(a + 1) * DM], ehT[:, e % 2, c, a * CAPH:(a + 1) * CAPH],
                                              w2_ring[:, e % RING, c, :], start=(c == 0), stop=(c == HC - 1))
                mm.then_inc(ey_done, 1)

            pe.wait_ge(logits_saved, CHUNKS)
            pe.wait_ge(slots_ready, 2)
            expert_rows(0)
            for e in range(EXPERTS):
                if e + 1 < EXPERTS:
                    expert_rows(e + 1)
                expert_up(e)
                if e:
                    expert_down(e - 1)
            expert_down(EXPERTS - 1)

            pe.wait_ge(relu_done, 2 * EXPERTS)
            pe.wait_ge(y_saved, EXPERTS)
            pe.wait_ge(late_in, 16 * 6)
            walk(IN1)
            pe.wait_ge(q_saved[1], CHUNKS)
            pe.wait_ge(k_saved[1], CHUNKS)
            pe.wait_ge(v_saved[1], TILES)
            attention(1)
            pe.wait_ge(ff_in, 16 * 4)
            pe.wait_ge(ctx_done[1], ITERS)
            walk(OUT1)

        @block.vector
        def _(dve):
            first = 0

            def row_stats(n, c):
                for t in range(c * CH, (c + 1) * CH):
                    last = nc.vector.bn_stats(stats[:, t, :], x_sb[:, t, :])
                last.then_inc(stats_done, 1)
                dve.wait_ge(stats_done, n * CHUNKS + c + 1)
                for t in range(c * CH, (c + 1) * CH):
                    nc.vector.bn_aggr(ln_mv[:, t, :], stats[:, t, :]).then_inc(ln_step, 1)
                dve.wait_ge(ln_step, (CH + 1) * (n * CHUNKS + c) + CH)
                cs = slice(c * CH, (c + 1) * CH)
                nc.vector.tensor_scalar(ln_ve[:, cs], ln_mv[:, cs, 1], EPS, None, ALU.add).then_inc(ln_step, 1)

            def normalize(n, c):
                dve.wait_ge(rstd_done, n * CHUNKS + c + 1)
                for t in range(c * CH, (c + 1) * CH):
                    nc.vector.tensor_scalar(xn_all[:, t, :], x_sb[:, t, :], ln_mv[:, t, 0:1], ln_rstd[:, t:t + 1],
                                            ALU.subtract, ALU.mult).then_inc(normed, 1)

            def save_v(L, c, count):
                dve.wait_ge(proj_done[L], count)
                for t in range(CH):
                    dst = v_all[:, c * CH + t].rearrange("p g (j d) -> p g j d", d=HV)[:, :, :, 0:HD]
                    nc.vector.tensor_tensor(dst, ps_v[:, t * P:(t + 1) * P].rearrange("p (g j d) -> p g j d", g=GROUPS, j=JH),
                                            bv_b[L][:].rearrange("p (g j d) -> p g j d", g=GROUPS, j=JH), ALU.add).then_inc(v_saved[L], 1)

            def save_kv0(c):
                dve.wait_ge(proj_done[0], 3 * c + 2)
                nc.vector.tensor_scalar(qk_all[:, 1, c * CT:(c + 1) * CT], ps_k, bqk[0][:, 1:2], None, ALU.add).then_inc(k_saved[0], 1)
                save_v(0, c, 3 * c + 3)

            def save_qkv1(c):
                for i, p in enumerate((ps_k, ps_kr)):
                    dve.wait_ge(proj_done[1], 5 * c + 3 + i)
                    nc.vector.tensor_scalar(rope_t[:, i, 1, :], p, bqk[1][:, 2 * i + 1:2 * i + 2], None, ALU.add).then_inc(rope_step, 1)
                save_v(1, c, 5 * c + 5)
                dve.wait_ge(rope_q, 2 * c + 2)
                dve.wait_ge(rope_step, 6 * c + 2)
                for i, f in enumerate((cos_t, sin_t)):
                    nc.vector.tensor_tensor(rope_t[:, i], rope_t[:, i], f[:].unsqueeze(1).to_broadcast([P, 2, CT]), ALU.mult).then_inc(rope_step, 2)
                dve.wait_ge(rope_step, 6 * c + 6)
                nc.vector.tensor_tensor(qk_all[:, 1, c * CT:(c + 1) * CT], rope_t[:, 0, 1, :], rope_t[:, 1, 1, :], ALU.add).then_inc(k_saved[1], 1)
                nc.vector.tensor_tensor(qk_all[:, 0, c * CT:(c + 1) * CT], rope_t[:, 0, 0, :], rope_t[:, 1, 0, :], ALU.add).then_inc(q_saved[1], 1)

            def top_half(it, hp):
                s = s_sb[:, hp]
                dve.wait_ge(scores_saved, 2 * it + hp + 1)
                dve.sem_inc(top_step, 1)
                k = 1
                for r in range(ROUNDS):
                    src = s if r == 0 else rest
                    for u in range(4):
                        if r:
                            dve.wait_ge(top_step, k - 3)
                        nc.vector.max(top[:, u, 8 * r:8 * r + 8], src[:, u, :]).then_inc(top_step, 1)
                        k += 1
                    if r == 0:
                        dve.wait_ge(top_step, k)
                        nc.vector.tensor_scalar(negm[:, hp, :], top[:, :, 0], -SCALE, None, ALU.mult).then_inc(neg_done[0], 1)
                    if r < ROUNDS - 1:
                        for u in range(4):
                            dve.wait_ge(top_step, k - 3)
                            nc.vector.match_replace(rest[:, u, :], top[:, u, 8 * r:8 * r + 8], src[:, u, :], NEG).then_inc(top_step, 1)
                            k += 1
                dve.wait_ge(top_step, k)
                dve.sem_clear(top_step)
                for u in range(4):
                    dve.wait_ge(exp_done[0], 4 * (2 * it + hp) + u + 1)
                    nc.vector.scalar_tensor_tensor(out=e_sb[:, hp, u, :], in0=s[:, u, :], scalar=top[:, u, TOPU - 1:TOPU],
                                                   in1=e_sb[:, hp, u, :], op0=ALU.is_ge, op1=ALU.mult).then_inc(probs_done, 1)

            def max_half(it, hp):
                s = ps_scores(hp)
                dve.wait_ge(scores_done[1], 2 * it + hp + 1)
                nc.vector.tensor_reduce(top[:, :, hp], s, AX_X, ALU.max).then_inc(max_done, 1)
                dve.wait_ge(max_done, 2 * it + hp + 1)
                nc.vector.tensor_scalar(negm[:, hp, :], top[:, :, hp], -SCALE, None, ALU.mult).then_inc(neg_done[1], 1)

            def contexts(L, it):
                b, g = it // GROUPS, it % GROUPS
                dve.wait_ge(ctx_T[L], it + 1)
                v = ps_ctx.rearrange("p (q j d) -> p q j d", q=KT, j=JH)
                nc.vector.reciprocal(recip[:], v[:, :, :, HD]).then_inc(recip_done[L], 1)
                dve.wait_ge(recip_done[L], it + 1)
                dst = xn_all[:, bass.ds(b * KT, KT), bass.ds(g * JH * HD, JH * HD)].rearrange("p q (j d) -> p q j d", d=HD)
                nc.vector.tensor_tensor(dst, v[:, :, :, 0:HD], recip[:].unsqueeze(3).to_broadcast([P, KT, JH, HD]), ALU.mult)\
                    .then_inc(ctx_done[L], 1)

            def attention(L):
                half = top_half if L == 0 else max_half
                for it in range(2):
                    half(it, 0)
                    half(it, 1)
                with dve.Fori(2, ITERS) as it:
                    half(it, 0)
                    contexts(L, it - 2)
                    half(it, 1)
                contexts(L, ITERS - 2)
                contexts(L, ITERS - 1)

            def add_attention(L, c):
                dve.wait_ge(bias_added, (L * CHUNKS) + c + 1)
                dve.wait_ge(out_done[L], c + 1)
                xs = x_sb[:, c * CH:(c + 1) * CH, :]
                nc.vector.tensor_tensor(xs, xs, ps_out.rearrange("p (t d) -> p t d", d=DM), ALU.add).then_inc(res_done[L], 1)
                dve.wait_ge(res_done[L], c + 1)
                row_stats(2 * L + 1, c)

            nc.vector.memset(ones_b[:], 1.0).then_inc(setup_dve, 1)
            nc.vector.memset(zero_rows[:], 0.0).then_inc(setup_dve, 1)
            for c in range(CHUNKS + 2):
                if c < CHUNKS:
                    dve.wait_ge(x_in[c], 16)
                    row_stats(0, c)
                if 1 <= c <= CHUNKS:
                    normalize(0, c - 1)
                if c == 1:
                    dve.wait_ge(consts_in, 16 * 6)
                if c >= 2:
                    save_kv0(c - 2)
            attention(0)
            dve.wait_ge(route_in, 16 * 4)
            nc.vector.tensor_copy(triu_b[:], triu[:]).then_inc(setup_dve, 1)
            for c in range(CHUNKS):
                add_attention(0, c)
                if c:
                    normalize(1, c - 1)
            normalize(1, CHUNKS - 1)

            steps = [0]

            def step(ins):
                ins.then_inc(rstep, 1)
                steps[0] += 1
                dve.wait_ge(rstep, steps[0])

            def col(a):
                return a.unsqueeze(2).to_broadcast([P, TILES, EXPERTS])

            lmax, who, esum, prob, place, keep, slot, tmp, weight = (rs[:, i, :] for i in range(9))
            dve.wait_ge(logits_saved, CHUNKS)
            step(nc.vector.tensor_reduce(lmax, logits[:], AX_X, ALU.max))
            step(nc.vector.tensor_tensor(rt[:, 0], logits[:], col(lmax), ALU.subtract))
            step(nc.vector.tensor_scalar(rt[:, 2], rt[:, 0], 0.0, None, ALU.is_ge))
            step(nc.vector.tensor_tensor(rt[:, 2], rt[:, 2], rev[:], ALU.mult))
            step(nc.vector.tensor_reduce(who, rt[:, 2], AX_X, ALU.max))
            step(nc.vector.tensor_tensor(rt[:, 3], rt[:, 2], col(who), ALU.is_equal))
            nc.vector.tensor_copy(mask_b[:], rt[:, 3]).then_inc(mask_done, 1)
            dve.wait_ge(gate_exp, 1)
            step(nc.vector.tensor_reduce(esum, rt[:, 1], AX_X, ALU.add))
            step(nc.vector.reciprocal(prob, esum))
            dve.wait_ge(cum_done, 1)
            step(nc.vector.tensor_tensor(rt[:, 0], rt[:, 3], ps[:, 6, 0:ER].rearrange("p (t e) -> p t e", e=EXPERTS), ALU.mult))
            step(nc.vector.tensor_reduce(place, rt[:, 0], AX_X, ALU.add))
            step(nc.vector.tensor_scalar(keep, place, float(CAP), None, ALU.is_le))
            step(nc.vector.tensor_scalar(tmp, who, -float(CAP), float(EXPERTS * CAP - 1), ALU.mult, ALU.add))
            step(nc.vector.tensor_tensor(slot, tmp, place, ALU.add))
            step(nc.vector.tensor_tensor(tmp, slot, spill[:], ALU.subtract))
            step(nc.vector.tensor_tensor(tmp, tmp, keep, ALU.mult))
            nc.vector.tensor_tensor(slot_idx[:], tmp, spill[:], ALU.add).then_inc(slots_ready, 1)
            nc.vector.tensor_tensor(back_idx[:], slot, keep, ALU.mult).then_inc(slots_ready, 1)
            step(nc.vector.tensor_tensor(weight, prob, keep, ALU.mult))

            for e in range(EXPERTS):
                for bank in range(2):
                    dve.wait_ge(eh_done, 2 * e + bank + 1)
                    if e >= 2:
                        dve.wait_ge(ey_done, e - 1)
                    nc.vector.tensor_scalar(ehT[:, e % 2, 2 * bank:2 * bank + 2, :].rearrange("p c n -> p (c n)"),
                                            ps[:, 2 + 2 * (e % 2) + bank, 0:2 * CAP], 0.0, None, ALU.max).then_inc(relu_done, 1)
            def add_moe(c):
                dve.wait_ge(gathered[c], 16 * CH)
                for t in range(c * CH, (c + 1) * CH):
                    nc.vector.scalar_tensor_tensor(out=x_sb[:, t, :], in0=xn_all[:, t, :], scalar=weight[:, t:t + 1], in1=x_sb[:, t, :],
                                                   op0=ALU.mult, op1=ALU.add).then_inc(moe_added, 1)
                dve.wait_ge(moe_added, CH * (c + 1))
                row_stats(2, c)

            for c in range(CHUNKS + 2):
                if c < CHUNKS:
                    add_moe(c)
                if 1 <= c <= CHUNKS:
                    normalize(2, c - 1)
                if c == 1:
                    dve.wait_ge(late_in, 16 * 6)
                if c >= 2:
                    save_qkv1(c - 2)
            attention(1)
            dve.wait_ge(ff_in, 16 * 4)

            def save_hidden(c):
                for i in range(2, HC):
                    dve.wait_ge(h_done, HC * c + i + 1)
                    nc.vector.tensor_scalar(hT[:, c % 2, i, :], ps[:, 4 + i, :], ffb1_sb[:, i:i + 1], 0.0, ALU.add, ALU.max).then_inc(h_saved_v, 1)

            def add_mlp(c):
                dve.wait_ge(bias_added, 2 * CHUNKS + c + 1)
                dve.wait_ge(ff_done, c + 1)
                xs = x_sb[:, c * CH:(c + 1) * CH, :]
                nc.vector.tensor_tensor(xs, xs, ps_down.rearrange("p (t d) -> p t d", d=DM), ALU.add).then_inc(added, 1)

            for c in range(CHUNKS + 3):
                if c < CHUNKS:
                    add_attention(1, c)
                if 1 <= c <= CHUNKS:
                    normalize(3, c - 1)
                if 2 <= c <= CHUNKS + 1:
                    save_hidden(c - 2)
                if c >= 3:
                    add_mlp(c - 3)


def kernel(**inputs):
    import numpy as np
    import concourse.bacc as bacc
    from concourse.bass_utils import run_bass_kernel_spmd

    a = {k: np.asarray(v) for k, v in inputs.items()}
    f32 = np.float32
    swap = np.arange(DM) ^ 1

    def columns(*rows):
        return np.ascontiguousarray(np.stack(rows, axis=1))

    d = np.arange(DM) % HD
    inv_freq = (f32(1.0) / f32(10000.0) ** (np.arange(0, HD, 2, dtype=f32) / f32(HD))).astype(f32)
    angle = (inv_freq[d % (HD // 2)][:, None] * np.tile(np.arange(SEQ, dtype=f32), CT // SEQ)[None, :]).astype(f32)
    sign = np.where(d % 2 == 0, f32(-1), f32(1))[:, None]
    token = np.arange(TILES, dtype=f32)[None, :] * P + np.arange(P, dtype=f32)[:, None]
    arrays = {
        "x": a["L0_attn_x"],
        "w0": columns(*(a[f"L0_attn_W{n}"].T for n in "qkvo")),
        "bqk0": columns(a["L0_attn_bq"], a["L0_attn_bk"]),
        "bv0": a["L0_attn_bv"],
        "bo0": a["L0_attn_bo"],
        "gate": a["L0_ffn_gate_w"].T,
        "w1": a["L0_ffn_w1"],
        "w2": a["L0_ffn_w2"],
        "w5": columns(*(a[f"L1_attn_W{n}"].T for n in "qkvo"), a["L1_attn_Wq"][swap].T, a["L1_attn_Wk"][swap].T),
        "bqk1": columns(a["L1_attn_bq"], a["L1_attn_bk"], a["L1_attn_bq"][swap], a["L1_attn_bk"][swap]),
        "bv1": a["L1_attn_bv"],
        "bo1": a["L1_attn_bo"],
        "ffw1": a["L1_ffn_W1"],
        "ffb1": a["L1_ffn_b1"].reshape(HC, P).T,
        "ffw2": a["L1_ffn_W2"],
        "ffb2": a["L1_ffn_b2"],
        "ident_d": np.eye(P, dtype=f32),
        "hmask_d": (np.arange(DM)[:, None] // HD == np.arange(HEADS)[None, :]).astype(f32),
        "cos_d": np.cos(angle).astype(f32),
        "sin_d": (sign * np.sin(angle)).astype(f32),
        "triu_d": np.triu(np.ones((P, P), dtype=f32)),
        "rev_d": np.broadcast_to(EXPERTS - np.arange(EXPERTS, dtype=f32), (P, TILES, EXPERTS)),
        "spill_d": token + f32(SLOTS),
    }
    arrays = {k: np.ascontiguousarray(v) for k, v in arrays.items()}
    nc = bacc.Bacc("TRN2", target_bir_lowering=False, num_devices=1)
    args = {k: nc.dram_tensor(f"in_{k}", v.shape, F32, kind="ExternalInput").ap() for k, v in arrays.items()}
    out = nc.dram_tensor("out_0", (BATCH, SEQ, DM), F32, kind="ExternalOutput").ap()
    build(nc, out=out, **args)
    r = run_bass_kernel_spmd(nc, [{f"in_{k}": v for k, v in arrays.items()}], core_ids=[0])
    return r.results[0]["out_0"]
```

```python
from contextlib import ExitStack

import concourse.bass as bass
from concourse import mybir

F32 = mybir.dt.float32
BF16 = mybir.dt.bfloat16
U32 = mybir.dt.uint32
ALU = mybir.AluOpType
ACT = mybir.ActivationFunctionType
AX_X = mybir.AxisListType.X

P = 128
BATCH, SEQ, DM = 8, 256, 128
HEADS = 16
HD = DM // HEADS
HV = HD + 1
TILES = BATCH * SEQ // P
TOKENS = TILES * P
CH = 4
CHUNKS = TILES // CH
CT = CH * P
KT = SEQ // P
GROUPS = 4
JH = HEADS // GROUPS
ITERS = BATCH * GROUPS
VW = JH * HV
TOPU = 27
ROUNDS = 4
MASKED = 1024.0
SCALE = HD ** -0.5
EPS = 1e-5
NEG = -3.0e38
EXPERTS, HID = 16, 512
HC = HID // P
CAP = 160
CAPH = CAP // 2
SLOTS = EXPERTS * CAP
RING = 8
XB = 4
ER = TILES * EXPERTS
PARTS = 3
STACK = PARTS * PARTS * HD


def build(nc, x, w0, bqk0, bv0, bo0, gate, w1, w2, w5, bqk1, bv1, bo1, ffw1, ffb1, ffw2, ffb2,
          ident_d, neg_ident_d, hmask_d, cos_d, sin_d, triu_d, rev_d, spill_d, out):
    with ExitStack() as ctx:
        def sb(name, shape, dt=F32):
            return ctx.enter_context(nc.sbuf_tensor(name, shape, dt))

        def sem(name):
            return ctx.enter_context(nc.semaphore(name))

        def pair(name):
            return [sem(f"{name}0"), sem(f"{name}1")]

        dispatched = nc.dram_tensor("dispatched", (SLOTS + TOKENS, DM), F32, kind="Internal").ap()
        parts_d = nc.dram_tensor("parts_d", (BATCH, 2, PARTS, HD, HEADS * SEQ), BF16, kind="Internal").ap()
        expert_out = nc.dram_tensor("expert_out", (SLOTS, DM), F32, kind="Internal").ap()

        ident = sb("ident", [P, P])
        neg_half = sb("neg_half", [P, TILES])
        warm = sb("warm", [P, 1])
        hmask = sb("hmask", [P, HEADS])
        wqkvo = [sb("wqkvo0", [P, 4, DM]), sb("wqkvo1", [P, 6, DM])]
        bqk = [sb("bqk0_sb", [P, 2]), sb("bqk1_sb", [P, 4])]
        bv_b = [sb("bv0_sb", [P, DM]), sb("bv1_sb", [P, DM])]
        bo_b = [sb("bo0_sb", [P, DM]), sb("bo1_sb", [P, DM])]
        cos_t = sb("cos_t", [P, CT])
        sin_t = sb("sin_t", [P, CT])
        gate_sb = sb("gate_sb", [P, EXPERTS])
        triu = sb("triu", [P, P])
        zero_rows = sb("zero_rows", [P, DM])
        triu_b = sb("triu_b", [P, P], BF16)
        ones_b = sb("ones_b", [P, P], BF16)
        rev = sb("rev", [P, TILES, EXPERTS])
        spill = sb("spill", [P, TILES])
        ffw1_sb = sb("ffw1_sb", [P, HID])
        ffw2_sb = sb("ffw2_sb", [P, HC, DM])
        ffb1_sb = sb("ffb1_sb", [P, HC])
        ffb2_b = sb("ffb2_b", [P, DM])
        ring = sb("ring", [P, 2, RING * HID])
        w1_ring = ring[:, 0, :].rearrange("p (r h) -> p r h", r=RING)
        w2_ring = ring[:, 1, :].rearrange("p (r c d) -> p r c d", r=RING, c=HC)
        stack = ring[:].rearrange("p a n -> p (a n)").bitcast(BF16).rearrange("p (r n) -> p r n", n=SEQ)
        x_sb = sb("x_sb", [P, TILES, DM])
        xn_all = sb("xn_all", [P, TILES, DM])
        stats = sb("stats", [P, TILES, 6])
        ln_mv = sb("ln_mv", [P, TILES, 2])
        ln_ve = sb("ln_ve", [P, TILES])
        ln_rstd = sb("ln_rstd", [P, TILES])
        rowsT = sb("rowsT", [P, 2, CT])
        rope_t = sb("rope_t", [P, 2, 2, CT])
        qk_all = sb("qk_all", [P, 2, TOKENS])
        q_st = sb("q_st", [P, JH, SEQ])
        v_all = sb("v_all", [P, TILES, GROUPS, VW])
        v_st = sb("v_st", [P, KT, JH, 32])
        ot_sb = sb("ot_sb", [P, SEQ])
        top = sb("top", [P, 2, 4, 8 * ROUNDS])
        peak = sb("peak", [P, 2, 4])
        rest = sb("rest", [P, 4, SEQ])
        mask = sb("mask", [P, 2, 4, SEQ])
        k_st = sb("k_st", [P, JH, SEQ])
        neg_ident = sb("neg_ident", [P, P])
        row_max = sb("row_max", [P, 4, 2])
        negm = sb("negm", [P, 2, 4])
        s_sb = sb("s_sb", [P, 2, 4, SEQ])
        e_sb = sb("e_sb", [P, 2, 4, SEQ])
        pt_sb = sb("pt_sb", [P, 2, 2, KT, SEQ])
        recip = sb("recip", [P, KT, JH])
        hT = sb("hT", [P, 2, HC, CT])
        rope = [e_sb[:].rearrange("p a b n -> p (a b n)").rearrange("p (i j n) -> p i j n", i=2, j=2), rope_t]
        parts = [hT[:, s].rearrange("p c n -> p (c n)").bitcast(BF16).rearrange("p (a i n) -> p a i n", i=2, n=CT) for s in range(2)]
        left = s_sb[:, 0].rearrange("p u n -> p (u n)").rearrange("p (i n) -> p i n", i=2)
        logits = sb("logits", [P, TILES, EXPERTS])
        rt = sb("rt", [P, 4, TILES, EXPERTS])
        mask_b = sb("mask_b", [P, TILES, EXPERTS], BF16)
        rs = sb("rs", [P, 9, TILES])
        slot_idx = sb("slot_idx", [P, TILES], U32)
        back_idx = sb("back_idx", [P, TILES], U32)
        xg = sb("xg", [CAPH, 2, XB * 2, DM])
        y_sb = sb("y_sb", [CAPH, RING, 2, DM])
        ehT = sb("ehT", [P, 2, HC, CAP])
        xeT = sb("xeT", [P, 2, CAP])
        yT = sb("yT", [P, 2, CAP])

        ps = ctx.enter_context(nc.psum_tensor("ps", [P, 8, 512], F32))

        x_in = [sem(f"x_in{c}") for c in range(CHUNKS)]
        consts_in, late_in, route_in, ff_in = sem("consts_in"), sem("late_in"), sem("route_in"), sem("ff_in")
        setup_done = sem("setup_done")
        setup_dve = sem("setup_dve")
        stats_done = sem("stats_done")
        ln_step = sem("ln_step")
        rstd_done = sem("rstd_done")
        normed = sem("normed")
        bias_added = sem("bias_added")
        rows_T = sem("rows_T")
        rowsT_saved = sem("rowsT_saved")
        proj_done = pair("proj_done")
        q_saved, k_saved, v_saved = pair("q_saved"), pair("k_saved"), pair("v_saved")
        rope_in = sem("rope_in")
        rope_step_q, rope_step_k = sem("rope_step_q"), sem("rope_step_k")
        q_staged, v_staged = sem("q_staged"), pair("v_staged")
        scores_done = pair("scores_done")
        k_staged = sem("k_staged")
        top_step = sem("top_step")
        peak_done, tops_done, mask_go = sem("peak_done"), sem("tops_done"), sem("mask_go")
        masked = sem("masked")
        max_done = sem("max_done")
        neg_done = sem("neg_done")
        exp_done = sem("exp_done")
        scores_saved = sem("scores_saved")
        probs_T = pair("probs_T")
        pt_done = pair("pt_done")
        pt_done_v = sem("pt_done_v")
        pv_done = pair("pv_done")
        ot_saved = pair("ot_saved")
        ctx_T = pair("ctx_T")
        recip_done, ctx_done = pair("recip_done"), pair("ctx_done")
        out_done, res_done = pair("out_done"), pair("res_done")
        logits_done, logits_saved = sem("logits_done"), sem("logits_saved")
        rstep = sem("rstep")
        gate_exp = sem("gate_exp")
        mask_done = sem("mask_done")
        cum_done = sem("cum_done")
        slots_ready = sem("slots_ready")
        zeroed = sem("zeroed")
        scattered = sem("scattered")
        xg_in = [sem(f"xg_in{s}") for s in range(2)]
        w_in = [sem(f"w_in{r}") for r in range(RING)]
        w_again = [sem(f"w_again{r}") for r in range(RING)]
        xe_T, xeT_done = sem("xe_T"), sem("xeT_done")
        eh_done, relu_done = sem("eh_done"), sem("relu_done")
        ey_done, yT_saved = sem("ey_done"), sem("yT_saved")
        y_turned, y_saved = sem("y_turned"), sem("y_saved")
        y_out = [sem(f"y_out{r}") for r in range(RING)]
        gathered = [sem(f"gathered{c}") for c in range(CHUNKS)]
        moe_added = sem("moe_added")
        h_done, h_saved_a, h_saved_v = sem("h_done"), sem("h_saved_a"), sem("h_saved_v")
        ff_done, added = sem("ff_done"), sem("added")
        part_made, left_made, parts_out, stack_zeroed, stack_in = (sem(n) for n in (
            "part_made", "left_made", "parts_out", "stack_zeroed", "stack_in"))
        stored = sem("stored")

        block = ctx.enter_context(nc.Block())

        ps_q, ps_k, ps_v, ps_qr, ps_kr = (ps[:, i, :] for i in range(2, 7))
        ps_down = ps[:, 3, :]

        def ps_T(m):
            return ps[:, m % 2, :]

        def ps_qkv0(c):
            own, other = c % 2, 1 - c % 2
            return [ps[:, i, :] for i in ((2, 3, 4) if c == 0 else (other, own, other))]

        def ps_out(L):
            return ps[:, 2 if L else 1, :]

        ps_logits = ps[:, 0, 0:CH * EXPERTS]

        ps_scores0 = ps[:, 2:4, :].rearrange("p a (b n) -> p (a b) n", b=KT)

        def ps_scores(hp):
            return ps[:, 2 * hp:2 * hp + 2, :].rearrange("p a (b n) -> p (a b) n", b=KT)

        ps_o = ps[:, 6, 0:SEQ]
        ps_ctx = ps[:, 7, 0:SEQ]

        def staggered(a, b):
            order = [(a, 0), (a, 1)] + [e for c in range(2, CHUNKS) for e in ((a, c), (b, c - 2))]
            return order + [(b, CHUNKS - 2), (b, CHUNKS - 1)]

        IN0 = [("qkv0", c) for c in range(CHUNKS)]
        OUT0 = [e for c in range(CHUNKS) for e in (("out0", c), ("gates", c))]
        IN1 = [("qkv1", c) for c in range(CHUNKS)]
        OUT1 = staggered("out1", "mlp")
        AT = {e: m for m, e in enumerate(IN0 + OUT0 + IN1 + OUT1)}
        LEAD = 3
        OUT_LAG = 3
        OUT_AT = [(c + 1) * ITERS // CHUNKS - 1 + OUT_LAG for c in range(CHUNKS - 1)]
        LOOPS = list(zip([LEAD] + [i + 2 for i in OUT_AT], OUT_AT + [ITERS - 1]))
        NORMS = {"qkv0": 0, "gates": 1, "qkv1": 2, "mlp": 3}

        def mask_unit(engine, hp, u):
            engine.tensor_scalar(mask[:, hp, u, :], s_sb[:, hp, u, :], top[:, hp, u, TOPU - 1:TOPU], peak[:, hp, u:u + 1],
                                 ALU.is_lt, ALU.add).then_inc(masked, 1)

        def rotate(engine, queue, c, j, step, done):
            r = rope[c % 2]
            queue.wait_ge(rope_in, 4 * c + 2 * j + 2)
            for i, f in enumerate((cos_t, sin_t)):
                engine.tensor_tensor(r[:, i, j, :], r[:, i, j, :], f[:], ALU.mult).then_inc(step, 1)
            queue.wait_ge(step, 2 * c + 2)
            engine.tensor_tensor(qk_all[:, j, c * CT:(c + 1) * CT], r[:, 0, j, :], r[:, 1, j, :], ALU.add).then_inc(done, 1)

        @block.sync
        def _(sp):
            rows = x.rearrange("b (t p) d -> p (b t) d", p=P)
            for c in range(CHUNKS):
                sp.dma_start(x_sb[:, c * CH:(c + 1) * CH, :], rows[:, c * CH:(c + 1) * CH, :]).then_inc(x_in[c], 16)
            for dst, src in ((ident[:], ident_d), (neg_ident[:], neg_ident_d), (hmask[:], hmask_d), (wqkvo[0][:], w0), (bqk[0][:], bqk0),
                             (bv_b[0][:], bv0.partition_broadcast(P)), (bo_b[0][:], bo0.partition_broadcast(P))):
                sp.dma_start(dst, src).then_inc(consts_in, 16)
            for dst, src in ((wqkvo[1][:], w5), (bqk[1][:], bqk1), (bv_b[1][:], bv1.partition_broadcast(P)),
                             (bo_b[1][:], bo1.partition_broadcast(P)), (cos_t[:], cos_d), (sin_t[:], sin_d)):
                sp.dma_start(dst, src).then_inc(late_in, 16)
            for dst, src in ((gate_sb[:], gate), (triu[:], triu_d), (rev[:], rev_d), (spill[:], spill_d)):
                sp.dma_start(dst, src).then_inc(route_in, 16)
            for dst, src in ((ffw1_sb[:], ffw1), (ffw2_sb[:], ffw2.rearrange("(c p) d -> p c d", p=P)),
                             (ffb1_sb[:], ffb1), (ffb2_b[:], ffb2.partition_broadcast(P))):
                sp.dma_start(dst, src).then_inc(ff_in, 16)
            for r in range(RING):
                sp.dma_start(w1_ring[:, r], w1[r]).then_inc(w_in[r], 16)
                sp.dma_start(w2_ring[:, r], w2[r].rearrange("(c p) d -> p c d", p=P)).then_inc(w_in[r], 16)
            sp.wait_ge(setup_dve, 2)
            sp.dma_start(dispatched[0:SLOTS, :].rearrange("(a p) d -> p a d", p=P), zero_rows[:].unsqueeze(1).to_broadcast([P, SLOTS // P, DM])).then_inc(zeroed, 16)
            sp.wait_ge(scattered, 16 * TILES)

            def load_rows(i, s):
                e0 = i * RING + s * XB
                sp.dma_start(xg[:, s], dispatched[bass.ds(e0 * CAP, XB * CAP), :].rearrange("(a p) d -> p a d", p=CAPH))\
                    .then_inc(xg_in[s], 16)

            def store_rows(i, r):
                e = i * RING + r
                sp.wait_ge(y_saved, i * RING + r + 1)
                sp.dma_start(expert_out[bass.ds(e * CAP, CAP), :].rearrange("(a p) d -> p a d", p=CAPH), y_sb[:, r])\
                    .then_inc(y_out[r], 16)

            load_rows(0, 0)
            load_rows(0, 1)
            for r in range(RING):
                if r % XB == XB - 2:
                    sp.wait_ge(xe_T, r + 2)
                    load_rows(1, r // XB)
                store_rows(0, r)
            for r in range(RING):
                store_rows(1, r)
            sp.wait_ge(stack_zeroed, 2 * RING)
            for c in range(CHUNKS):
                for b in (2 * c, 2 * c + 1):
                    for a in range(PARTS):
                        sp.wait_ge(part_made, PARTS * c + a + 1)
                        for i in range(2):
                            sp.dma_start(parts_d[b, i, a].rearrange("d (h t) -> h d t", h=HEADS),
                                         parts[c % 2][:, a, i, b % 2 * SEQ:(b % 2 + 1) * SEQ]).then_inc(parts_out, 16)
                    sp.wait_ge(parts_out, 16 * 2 * PARTS * (b + 1))
                    if b >= 2:
                        sp.wait_ge(scores_done[1], 2 * GROUPS * (b - 1))
                    if b:
                        sp.wait_ge(stack_in, 16 * 4 * b)
                    rows = b % 2 * 2 * HEADS
                    for a in range(PARTS):
                        sp.dma_start(stack[a * STACK // PARTS:(a + 1) * STACK // PARTS, rows:rows + HEADS, :],
                                     parts_d[b, 0, a].unsqueeze(0).to_broadcast([PARTS, HD, HEADS * SEQ])).then_inc(stack_in, 16)
                    sp.dma_start(stack[0:STACK, rows + HEADS:rows + 2 * HEADS, :],
                                 parts_d[b, 1].rearrange("a d n -> (a d) n").unsqueeze(0).to_broadcast([PARTS, PARTS * HD, HEADS * SEQ]))\
                        .then_inc(stack_in, 16)
            with sp.Fori(0, CHUNKS) as c:
                sp.wait_ge(added, c + 1)
                sp.dma_start(out.rearrange("b (t p) d -> p (b t) d", p=P)[:, bass.ds(c * CH, CH), :],
                             x_sb[:, bass.ds(c * CH, CH), :]).then_inc(stored, 16)
            sp.wait_ge(stored, 16 * CHUNKS)

        @block.gpsimd
        def _(pool):
            nc.gpsimd.memset(neg_half[:], -0.5).then_inc(setup_done, 1)
            nc.gpsimd.memset(v_st[:], 0.0).then_inc(setup_done, 1)
            nc.gpsimd.memset(v_all[:], 1.0).then_inc(setup_done, 1)

            def rstd(n, c):
                pool.wait_ge(ln_step, (CH + 1) * (n * CHUNKS + c + 1))
                if n == 0 and c == 0:
                    pool.wait_ge(setup_done, 1)
                cs = slice(c * CH, (c + 1) * CH)
                nc.gpsimd.tensor_tensor(ln_rstd[:, cs], ln_ve[:, cs], neg_half[:, cs], ALU.pow).then_inc(rstd_done, 1)

            def add_bias(n, c, bias):
                pool.wait_ge(normed, CH * (n * CHUNKS + c + 1))
                xs = x_sb[:, c * CH:(c + 1) * CH, :]
                nc.gpsimd.tensor_tensor(xs, xs, bias[:].unsqueeze(1).to_broadcast([P, CH, DM]), ALU.add).then_inc(bias_added, 1)

            def spread(dst, i, it, hp):
                b, g = it // GROUPS, it % GROUPS
                src = qk_all[:, i, bass.ds(b * SEQ, SEQ)].unsqueeze(1).to_broadcast([P, 2, SEQ])
                m = hmask[:, bass.ds(g * JH + 2 * hp, 2)].unsqueeze(2).to_broadcast([P, 2, SEQ])
                return nc.gpsimd.tensor_tensor(dst[:, 2 * hp:2 * hp + 2, :], src, m, ALU.mult)

            def stage_q(it, hp):
                if it is not first:
                    pool.wait_ge(scores_done[0], 2 * it + hp - 1)
                spread(q_st, 0, it, hp).then_inc(q_staged, 1)

            def leave(c, a):
                pool.wait_ge(part_made, PARTS * c + a + 1)
                whole = qk_all[:, :, c * CT:(c + 1) * CT] if a == 0 else left
                nc.gpsimd.tensor_tensor(left, whole, parts[c % 2][:, a], ALU.subtract).then_inc(left_made, 1)

            def stage_k(it, hp):
                if it is not first:
                    pool.wait_ge(probs_T[0], 2 * (2 * it + hp - 1))
                spread(k_st, 1, it, hp).then_inc(k_staged, 1)

            def masks(it, hp):
                n = 2 * it + hp
                pool.wait_ge(peak_done, n + 1)
                if it is not first:
                    pool.wait_ge(probs_T[0], 2 * (n - 1))
                pool.wait_ge(tops_done, 4 * n + 4)
                pool.sem_inc(mask_go, 1)
                for u in range(4):
                    mask_unit(nc.gpsimd, hp, u)

            def stage_v(L, it):
                b, g = it // GROUPS, it % GROUPS
                if it is not first:
                    pool.wait_ge(pv_done[L], 2 * it)
                nc.gpsimd.tensor_copy(
                    v_st[:, :, :, 0:HV],
                    v_all[:, bass.ds(b * KT, KT), bass.ds(g, 1), :].rearrange("p t a (j d) -> p t (a j) d", d=HV),
                ).then_inc(v_staged[L], 1)

            first = 0

            def serve0():
                pool.wait_ge(q_saved[0], 1)

                def half(it, hp, values, following):
                    if following is not None:
                        stage_q(following, hp)
                    stage_k(it, hp)
                    if values is not None and hp == 0:
                        stage_v(0, values)
                    masks(it, hp)

                def step(it):
                    half(it, 0, it - 1, it + 1)
                    half(it, 1, it - 1, it + 1)

                stage_q(first, 0)
                stage_q(first, 1)
                pool.wait_ge(k_saved[0], 1)
                pool.wait_ge(v_saved[0], CH)
                pool.wait_ge(setup_done, 3)
                for it in range(LEAD):
                    for hp in range(2):
                        n = 2 * it + hp
                        half(it, hp, it - 1 if it else None, it + 1)
                        if n + 2 < CHUNKS:
                            rstd(0, n + 2)
                        if n < CHUNKS:
                            add_bias(0, n, bo_b[0])
                pool.wait_ge(q_saved[0], CHUNKS)
                pool.wait_ge(k_saved[0], CHUNKS)
                pool.wait_ge(v_saved[0], TILES)
                for c, (start, end) in enumerate(LOOPS):
                    with pool.Fori(start, end) as it:
                        step(it)
                    if c < len(OUT_AT):
                        step(end)
                        step(end + 1)
                        rstd(1, c)
                half(ITERS - 1, 0, ITERS - 2, None)
                stage_k(ITERS - 1, 1)
                stage_v(0, ITERS - 1)

            def serve1():
                pool.wait_ge(q_saved[1], CHUNKS)
                pool.wait_ge(v_saved[1], TILES)

                stage_v(1, first)
                done = 2
                for c in range(1, CHUNKS):
                    for a in range(PARTS):
                        stage_v(1, done + a - 1)
                        if a:
                            leave(c, a - 1)
                    end = ITERS if c == CHUNKS - 1 else c * ITERS // CHUNKS
                    for t in range(c - 1, CHUNKS if c == CHUNKS - 1 else c):
                        add_bias(2, t, bo_b[1])
                    with pool.Fori(done + PARTS, end) as it:
                        stage_v(1, it - 1)
                    done = end
                stage_v(1, ITERS - 1)

            rstd(0, 0)
            rstd(0, 1)
            pool.wait_ge(consts_in, 16 * 7)
            serve0()
            rstd(1, CHUNKS - 1)
            pool.wait_ge(zeroed, 16)
            pool.wait_ge(slots_ready, 2)
            for t in range(TILES):
                pool.indirect_dma_start(dispatched[:, :], bass.IndirectOffsetOnAxis(slot_idx[:, t:t + 1], 0),
                                        xn_all[:, t, :], None).then_inc(scattered, 16)
            for r in range(RING):
                pool.wait_ge(ey_done, r + 1)
                pool.dma_start(w1_ring[:, r], w1[RING + r]).then_inc(w_again[r], 16)
                pool.dma_start(w2_ring[:, r], w2[RING + r].rearrange("(c p) d -> p c d", p=P)).then_inc(w_again[r], 16)
            for r in range(RING):
                pool.wait_ge(y_out[r], 16 * EXPERTS // RING)
            pool.wait_ge(scattered, 16 * TILES)
            for c in range(CHUNKS + 1):
                if c < CHUNKS:
                    for t in range(c * CH, (c + 1) * CH):
                        pool.indirect_dma_start(xn_all[:, t, :], None, expert_out[:, :],
                                                bass.IndirectOffsetOnAxis(back_idx[:, t:t + 1], 0)).then_inc(gathered[c], 16)
                if c:
                    rstd(2, c - 1)
            pool.wait_ge(late_in, 16 * 6)
            for c in range(CHUNKS):
                rotate(nc.gpsimd, pool, c, 0, rope_step_q, q_saved[1])
                if c == 0:
                    for a in range(PARTS - 1):
                        leave(0, a)
            serve1()
            pool.wait_ge(ff_in, 16 * 4)
            for c in range(CHUNKS):
                rstd(3, c)
                if c:
                    add_bias(3, c - 1, ffb2_b)
            add_bias(3, CHUNKS - 1, ffb2_b)

        @block.scalar
        def _(act):
            def save_rowsT(use, c):
                m = AT[use, c]
                act.wait_ge(rows_T, m + 1)
                nc.scalar.activation(rowsT[:, m % 2, :], ps_T(m), ACT.Copy).then_inc(rowsT_saved, 1)

            def save_q(c):
                act.wait_ge(proj_done[0], 3 * c + 1)
                nc.scalar.activation(qk_all[:, 0, c * CT:(c + 1) * CT], ps_qkv0(c)[0], ACT.Identity, bias=bqk[0][:, 0:1]).then_inc(q_saved[0], 1)

            def save_rope(c):
                if c >= 2:
                    act.wait_ge(q_saved[1], c - 1)
                    act.wait_ge(k_saved[1], c - 1)
                for n, (i, j, p) in enumerate(((0, 0, ps_q), (1, 0, ps_qr), (0, 1, ps_k), (1, 1, ps_kr))):
                    act.wait_ge(proj_done[1], 5 * c + 1 + n)
                    nc.scalar.activation(rope[c % 2][:, i, j, :], p, ACT.Identity, bias=bqk[1][:, 2 * i + j:2 * i + j + 1]).then_inc(rope_in, 1)

            def part(c, a):
                if a == 0:
                    act.wait_ge(q_saved[1], c + 1)
                    act.wait_ge(k_saved[1], c + 1)
                    if c >= 2:
                        act.wait_ge(parts_out, 16 * 4 * PARTS * (c - 1))
                else:
                    act.wait_ge(left_made, (PARTS - 1) * c + a)
                whole = qk_all[:, :, c * CT:(c + 1) * CT] if a == 0 else left
                nc.scalar.activation(parts[c % 2][:, a], whole, ACT.Copy).then_inc(part_made, 1)

            def save_logits(c):
                act.wait_ge(logits_done, c + 1)
                nc.scalar.activation(logits[:, c * CH:(c + 1) * CH, :], ps_logits.rearrange("p (t e) -> p t e", e=EXPERTS),
                                     ACT.Copy).then_inc(logits_saved, 1)

            def save_hidden(c):
                for i in range(2):
                    act.wait_ge(h_done, HC * c + i + 1)
                    nc.scalar.activation(hT[:, c % 2, i, :], ps[:, 4 + i, :], ACT.Relu, bias=ffb1_sb[:, i:i + 1]).then_inc(h_saved_a, 1)

            def walk(entries):
                for (use, c), following in zip(entries, entries[1:] + [None]):
                    if following:
                        save_rowsT(*following)
                    if use == "mlp":
                        save_hidden(c)

            def exps(it, hp):
                n = 2 * it + hp
                act.wait_ge(neg_done, n + 1)
                if it is not first:
                    act.wait_ge(probs_T[1], 2 * (n - 1))
                src = ps_scores(hp)
                for u in range(4):
                    nc.scalar.activation(e_sb[:, hp, u, :], src[:, u, :], ACT.Exp,
                                         bias=negm[:, hp, u:u + 1], scale=SCALE).then_inc(exp_done, 1)

            def save_scores(it, hp):
                act.wait_ge(scores_done[0], 2 * it + hp + 1)
                if it is not first:
                    act.wait_ge(masked, 4 * (2 * it + hp - 1))
                nc.scalar.activation(s_sb[:, hp], ps_scores0, ACT.Copy).then_inc(scores_saved, 1)

            def top_exps(it, hp):
                n = 2 * it + hp
                for jj in range(2):
                    act.wait_ge(probs_T[0], 2 * n + jj + 1)
                    if it is not first:
                        act.wait_ge(pv_done[0], n - 1)
                    nc.scalar.activation(pt_sb[:, hp, jj].rearrange("p a n -> p (a n)"), ps[:, 4 + jj, :], ACT.Exp, scale=SCALE)\
                        .then_inc(pt_done[0], 1)

            def attention0():
                second = 1

                def first_half(it):
                    save_scores(it, 0)
                    if it is not first:
                        top_exps(it - 1, 0)
                    if it is not first and it is not second:
                        save_ot(0, it - 2)

                def second_half(it):
                    save_scores(it, 1)
                    if it is not first:
                        top_exps(it - 1, 1)

                for n in range(2 * LEAD):
                    (second_half if n % 2 else first_half)(n // 2)
                    if 1 <= n - 1 < CHUNKS:
                        save_rowsT("qkv0", n - 1)
                        save_q(n - 1)
                for c, (start, end) in enumerate(LOOPS):
                    with act.Fori(start, end) as it:
                        first_half(it)
                        second_half(it)
                    first_half(end)
                    second_half(end)
                    if c:
                        save_rowsT("gates", c - 1)
                        save_logits(c - 1)
                    if c < len(OUT_AT):
                        first_half(end + 1)
                        second_half(end + 1)
                        save_rowsT("out0", c)
                top_exps(ITERS - 1, 0)
                save_ot(0, ITERS - 2)
                top_exps(ITERS - 1, 1)
                save_ot(0, ITERS - 1)

            def save_pt(it, hp):
                n = 2 * it + hp
                act.wait_ge(probs_T[1], 2 * n + 1)
                if it is not first:
                    act.wait_ge(pv_done[1], n - 1)
                nc.scalar.activation(pt_sb[:, hp, 0].rearrange("p a n -> p (a n)"), ps[:, 4, :], ACT.Copy).then_inc(pt_done[1], 1)

            def save_ot(L, it):
                act.wait_ge(pv_done[L], 2 * it + 2)
                if it is not first:
                    act.wait_ge(ctx_T[L], it)
                nc.scalar.activation(ot_sb[:], ps_o, ACT.Copy).then_inc(ot_saved[L], 1)

            first = 0

            def attention1():
                def step(it, prev, before_prev):
                    if before_prev is not None:
                        save_ot(1, before_prev)
                    exps(it, 0)
                    if prev is not None:
                        save_pt(prev, 1)
                    exps(it, 1)
                    save_pt(it, 0)

                step(first, None, None)
                step(1, first, None)
                done = 2
                for c in range(1, CHUNKS):
                    for a in range(PARTS):
                        step(done + a, done + a - 1, done + a - 2)
                        part(c, a)
                    end = ITERS if c == CHUNKS - 1 else c * ITERS // CHUNKS
                    with act.Fori(done + PARTS, end) as it:
                        step(it, it - 1, it - 2)
                    done = end
                save_ot(1, ITERS - 2)
                save_rowsT("out1", 0)
                save_pt(ITERS - 1, 1)
                save_rowsT("out1", 1)
                save_ot(1, ITERS - 1)

            act.wait_ge(setup_done, 1)
            nc.scalar.activation(warm[:], neg_half[:, 0:1], ACT.Exp)
            act.wait_ge(consts_in, 16 * 7)
            save_rowsT("qkv0", 0)
            save_q(0)
            attention0()
            save_rowsT("out0", CHUNKS - 1)
            save_rowsT("gates", CHUNKS - 1)
            save_logits(CHUNKS - 1)
            act.wait_ge(rstep, 2)
            nc.scalar.activation(rt[:, 1], rt[:, 0], ACT.Exp).then_inc(gate_exp, 1)

            def save_yT(e):
                act.wait_ge(ey_done, e + 1)
                if e >= 2:
                    act.wait_ge(y_turned, e - 1)
                nc.scalar.activation(yT[:, e % 2, :], ps[:, 6 + e % 2, 2 * DM:2 * DM + CAP], ACT.Copy).then_inc(yT_saved, 1)

            def save_y(e):
                act.wait_ge(y_turned, e + 1)
                if e >= RING:
                    act.wait_ge(y_out[e % RING], 16)
                nc.scalar.activation(y_sb[:, e % RING].rearrange("p a d -> p (a d)"),
                                     ps[0:CAPH, 6 + e % 2, 0:2 * DM], ACT.Copy).then_inc(y_saved, 1)

            for e in range(EXPERTS):
                act.wait_ge(xe_T, e + 1)
                if e >= 2:
                    act.wait_ge(eh_done, 2 * (e - 2) + 2)
                nc.scalar.activation(xeT[:, e % 2, :], ps[:, e % 2, 0:CAP], ACT.Copy).then_inc(xeT_done, 1)
                if e >= 2:
                    save_yT(e - 2)
                if e >= 3:
                    save_y(e - 3)
            save_yT(EXPERTS - 2)
            save_y(EXPERTS - 3)
            save_yT(EXPERTS - 1)
            save_y(EXPERTS - 2)
            save_y(EXPERTS - 1)
            act.wait_ge(late_in, 16 * 6)
            save_rowsT("qkv1", 0)
            save_rope(0)
            save_rowsT("qkv1", 1)
            save_rowsT("qkv1", 2)
            part(0, 0)
            save_rope(1)
            part(0, 1)
            save_rowsT("qkv1", 3)
            save_rope(2)
            part(0, 2)
            save_rope(3)
            act.wait_ge(q_saved[1], 3)
            act.wait_ge(k_saved[1], 3)
            attention1()
            act.wait_ge(ff_in, 16 * 4)
            walk(OUT1[1:])

        @block.tensor
        def _(pe):
            first = 0

            def turn_rows(use, c):
                m = AT[use, c]
                if use == "out1":
                    pe.wait_ge(ctx_done[1], (c + 1) * ITERS // CHUNKS)
                if use in NORMS:
                    pe.wait_ge(normed, CH * (NORMS[use] * CHUNKS + c + 1))
                if m >= 2:
                    pe.wait_ge(rowsT_saved, m - 1)
                for t in range(CH):
                    mm = nc.tensor.transpose(ps_T(m)[:, t * P:(t + 1) * P], xn_all[:, c * CH + t, :], ident[:])
                mm.then_inc(rows_T, 1)

            def qkv(L, c, rT, tile):
                w = wqkvo[L]
                if L and c:
                    pe.wait_ge(rope_in, 4 * c)
                    pe.wait_ge(v_saved[1], CH * c)
                q, k, v = (ps_q, ps_k, ps_v) if L else ps_qkv0(c)
                nc.tensor.matmul(q, w[:, 0, :], rT, start=True, stop=True).then_inc(proj_done[L], 1)
                if L == 1:
                    nc.tensor.matmul(ps_qr, w[:, 4, :], rT, start=True, stop=True).then_inc(proj_done[L], 1)
                nc.tensor.matmul(k, w[:, 1, :], rT, start=True, stop=True).then_inc(proj_done[L], 1)
                if L == 1:
                    nc.tensor.matmul(ps_kr, w[:, 5, :], rT, start=True, stop=True).then_inc(proj_done[L], 1)
                if L == 0 and c:
                    pe.wait_ge(q_saved[0], c + 1)
                for t in range(CH):
                    mm = nc.tensor.matmul(v[:, t * P:(t + 1) * P], tile(t), w[:, 2, :], start=True, stop=True)
                mm.then_inc(proj_done[L], 1)

            def project(L, c, tile):
                if L and c:
                    pe.wait_ge(res_done[1], c)
                for t in range(CH):
                    mm = nc.tensor.matmul(ps_out(L)[:, t * P:(t + 1) * P], tile(t), wqkvo[L][:, 3, :], start=True, stop=True)
                mm.then_inc(out_done[L], 1)

            def gates(c, tile):
                for t in range(CH):
                    mm = nc.tensor.matmul(ps_logits[:, t * EXPERTS:(t + 1) * EXPERTS], tile(t), gate_sb[:], start=True, stop=True)
                mm.then_inc(logits_done, 1)

            def beside(use, c):
                if use == "qkv0":
                    pe.wait_ge(k_saved[0], c)
                    pe.wait_ge(v_saved[0], CH * c)
                elif use == "out0":
                    if c:
                        pe.wait_ge(logits_saved, c)
                    pe.wait_ge(ctx_done[0], (c + 1) * ITERS // CHUNKS)
                elif use == "gates":
                    pe.wait_ge(res_done[0], c + 1)
                turn_rows(use, c)
                product(use, c)

            def mlp(c, rT):
                for i in range(HC):
                    if c:
                        pe.wait_ge(h_saved_a if i < 2 else h_saved_v, 2 * c)
                    nc.tensor.matmul(ps[:, 4 + i, :], ffw1_sb[:, i * P:(i + 1) * P], rT, start=True, stop=True).then_inc(h_done, 1)
                if c:
                    mlp_down(c - 1)
                if c == CHUNKS - 1:
                    mlp_down(c)

            def mlp_down(c):
                pe.wait_ge(h_saved_a, 2 * c + 2)
                pe.wait_ge(h_saved_v, 2 * c + 2)
                if c:
                    pe.wait_ge(added, c)
                for t in range(CH):
                    for i in range(HC):
                        mm = nc.tensor.matmul(ps_down[:, t * P:(t + 1) * P], hT[:, c % 2, i, t * P:(t + 1) * P], ffw2_sb[:, i, :],
                                              start=(i == 0), stop=(i == HC - 1))
                mm.then_inc(ff_done, 1)

            def product(use, c):
                m = AT[use, c]
                pe.wait_ge(rowsT_saved, m + 1)
                rT = rowsT[:, m % 2, :]

                def tile(t):
                    return rT[:, t * P:(t + 1) * P]

                if use in ("qkv0", "qkv1"):
                    qkv(int(use[3]), c, rT, tile)
                elif use in ("out0", "out1"):
                    project(int(use[3]), c, tile)
                elif use == "gates":
                    gates(c, tile)
                else:
                    mlp(c, rT)

            def walk(entries):
                for e, following in zip(entries, entries[1:] + [None]):
                    if following:
                        turn_rows(*following)
                    product(*e)

            def scores(L, it, hp):
                if L == 1 and hp == 0:
                    pe.wait_ge(stack_in, 16 * 4 * (it // GROUPS + 1))
                if L == 0:
                    pe.wait_ge(q_staged, 2 * it + hp + 1)
                    if not (it is first and hp == 0):
                        pe.wait_ge(scores_saved, 2 * it + hp)
                    dst = ps_scores0
                else:
                    if it is not first:
                        pe.wait_ge(exp_done, 4 * (2 * it + hp - 1))
                    dst = ps_scores(hp)
                b = it // GROUPS
                for jj in range(2):
                    if L == 0:
                        q, k = q_st[:, 2 * hp + jj, :], qk_all[:, 1, bass.ds(b * SEQ, SEQ)]
                    else:
                        row = b % 2 * (2 * HEADS) + it % GROUPS * JH + 2 * hp + jj
                        q, k = (stack[:, bass.ds(r, 1), :].rearrange("p a n -> p (a n)") for r in (row, row + HEADS))
                    for qt in range(KT):
                        mm = nc.tensor.matmul(dst[:, 2 * jj + qt, :], q[:, qt * P:(qt + 1) * P], k, start=True, stop=True)
                mm.then_inc(scores_done[L], 1)

            def masked_scores(it, hp):
                n = 2 * it + hp
                b = it // GROUPS
                pe.wait_ge(k_staged, n + 1)
                for jj in range(2):
                    if not (it is first and hp == 0):
                        pe.wait_ge(pt_done[0], 2 * n + jj - 1)
                    pe.wait_ge(masked, 4 * n + 2 * jj + 2)
                    for kt in range(KT):
                        out = ps[:, 4 + jj, kt * SEQ:(kt + 1) * SEQ]
                        nc.tensor.matmul(out, k_st[:, 2 * hp + jj, kt * P:(kt + 1) * P], qk_all[:, 0, bass.ds(b * SEQ, SEQ)],
                                         start=True, stop=False, skip_group_check=True)
                        for qt in range(KT):
                            mm = nc.tensor.matmul(out[:, qt * P:(qt + 1) * P], mask[:, hp, 2 * jj + qt, kt * P:(kt + 1) * P], neg_ident[:],
                                                  start=False, stop=(qt == KT - 1), skip_group_check=True)
                    mm.then_inc(probs_T[0], 1)

            def turn(it, hp):
                n = 2 * it + hp
                for jj in range(2):
                    pe.wait_ge(exp_done, 4 * n + 2 * jj + 2)
                    if not (it is first and hp == 0):
                        pe.wait_ge(pt_done_v if jj else pt_done[1], n)
                    for kt in range(KT):
                        for qt in range(KT):
                            mm = nc.tensor.transpose(ps[:, 4 + jj, kt * SEQ + qt * P:kt * SEQ + (qt + 1) * P],
                                                     e_sb[:, hp, 2 * jj + qt, kt * P:(kt + 1) * P], ident[:])
                    mm.then_inc(probs_T[1], 1)

            def sum_values(L, it, hp):
                n = 2 * it + hp
                if hp == 0:
                    pe.wait_ge(v_staged[L], it + 1)
                    if it is not first:
                        pe.wait_ge(ot_saved[L], it)
                if L == 0:
                    pe.wait_ge(pt_done[0], 2 * n + 2)
                else:
                    pe.wait_ge(pt_done[1], n + 1)
                    pe.wait_ge(pt_done_v, n + 1)
                for kt in range(KT):
                    for jj in range(2):
                        j = 2 * hp + jj
                        mm = nc.tensor.matmul(ps_o[32 * j:32 * j + 32, :], v_st[:, kt, j, :], pt_sb[:, hp, jj, kt, :],
                                              start=(kt == 0), stop=(kt == KT - 1), skip_group_check=True)
                mm.then_inc(pv_done[L], 1)

            def turn_back(L, it):
                pe.wait_ge(ot_saved[L], it + 1)
                if it is not first:
                    pe.wait_ge(ctx_done[L], it)
                for qt in range(KT):
                    mm = nc.tensor.transpose(ps_ctx[:, qt * P:(qt + 1) * P], ot_sb[:, qt * P:(qt + 1) * P], ident[:])
                mm.then_inc(ctx_T[L], 1)

            def attention0():
                second = 1

                def first_half(it):
                    scores(0, it, 0)
                    masked_scores(it - 1, 0)
                    if it is not second:
                        sum_values(0, it - 2, 1)

                def second_half(it, use=None, c=None):
                    scores(0, it, 1)
                    masked_scores(it - 1, 1)
                    sum_values(0, it - 1, 0)
                    if use:
                        beside(use, c)
                    if it is not second:
                        turn_back(0, it - 2)

                scores(0, first, 0)
                scores(0, first, 1)
                pe.wait_ge(v_saved[0], CH)
                first_half(second)
                beside("qkv0", 1)
                second_half(second)
                beside("qkv0", 2)
                first_half(2)
                beside("qkv0", 3)
                second_half(2)
                pe.wait_ge(k_saved[0], CHUNKS)
                pe.wait_ge(q_saved[0], CHUNKS)
                pe.wait_ge(route_in, 16 * 4)
                for c, (start, end) in enumerate(LOOPS):
                    with pe.Fori(start, end) as it:
                        first_half(it)
                        second_half(it)
                    first_half(end)
                    second_half(end, "gates" if c else None, c - 1)
                    if c < len(OUT_AT):
                        first_half(end + 1)
                        second_half(end + 1, "out0", c)
                masked_scores(ITERS - 1, 0)
                sum_values(0, ITERS - 2, 1)
                masked_scores(ITERS - 1, 1)
                sum_values(0, ITERS - 1, 0)
                turn_back(0, ITERS - 2)
                sum_values(0, ITERS - 1, 1)
                turn_back(0, ITERS - 1)

            def attention1():
                second, last = 1, ITERS - 1

                def first_step(it):
                    scores(1, it, 1)
                    turn(it - 1, 1)
                    if it is not second:
                        turn_back(1, it - 2)
                    sum_values(1, it - 1, 0)

                def second_step(it):
                    if it is not last:
                        scores(1, it + 1, 0)
                    if it is not first:
                        sum_values(1, it - 1, 1)
                    turn(it, 0)

                scores(1, first, 0)
                scores(1, first, 1)
                second_step(first)
                first_step(second)
                second_step(second)
                with pe.Fori(2, ITERS - 1) as it:
                    first_step(it)
                    second_step(it)
                first_step(last)
                second_step(last)
                turn_rows("out1", 0)
                turn(ITERS - 1, 1)
                turn_rows("out1", 1)
                product("out1", 0)
                turn_back(1, ITERS - 2)
                sum_values(1, ITERS - 1, 0)
                sum_values(1, ITERS - 1, 1)
                turn_back(1, ITERS - 1)

            pe.wait_ge(consts_in, 16 * 7)
            turn_rows("qkv0", 0)
            product("qkv0", 0)
            pe.wait_ge(q_saved[0], 1)
            pe.wait_ge(k_saved[0], 1)
            attention0()
            beside("out0", CHUNKS - 1)
            beside("gates", CHUNKS - 1)
            pe.wait_ge(mask_done, 1)
            pe.wait_ge(setup_dve, 3)
            flat = mask_b[:].rearrange("p t e -> p (t e)")
            nc.tensor.matmul(ps[:, 6, 0:ER], triu_b[:], flat, start=True, stop=False, skip_group_check=True)
            for t in range(1, TILES):
                mm = nc.tensor.matmul(ps[:, 6, t * EXPERTS:ER], ones_b[:], flat[:, 0:ER - t * EXPERTS], start=False,
                                      stop=(t == TILES - 1), skip_group_check=True)
            mm.then_inc(cum_done, 1)

            def expert_rows(e):
                s = (e // XB) % 2
                pe.wait_ge(xg_in[s], 16 * (e // RING + 1))
                if e >= 2:
                    pe.wait_ge(xeT_done, e - 1)
                for a in range(2):
                    mm = nc.tensor.transpose(ps[:, e % 2, a * CAPH:(a + 1) * CAPH], xg[:, s, 2 * (e % XB) + a, :], ident[0:CAPH, 0:CAPH])
                mm.then_inc(xe_T, 1)

            def expert_up(e):
                r = e % RING
                pe.wait_ge(w_in[r] if e < RING else w_again[r], 32)
                pe.wait_ge(xeT_done, e + 1)
                if e >= 2:
                    pe.wait_ge(relu_done, 2 * (e - 2) + 2)
                for bank in range(2):
                    for i in range(2):
                        c = 2 * bank + i
                        mm = nc.tensor.matmul(ps[:, 2 + 2 * (e % 2) + bank, i * CAP:(i + 1) * CAP],
                                              w1_ring[:, r, c * P:(c + 1) * P], xeT[:, e % 2, :], start=True, stop=True)
                    mm.then_inc(eh_done, 1)

            def expert_down(e):
                pe.wait_ge(relu_done, 2 * e + 2)
                if e >= 2:
                    pe.wait_ge(y_saved, e - 1)
                for c in range(HC):
                    mm = nc.tensor.matmul(ps[:, 6 + e % 2, 2 * DM:2 * DM + CAP], w2_ring[:, e % RING, c, :], ehT[:, e % 2, c, :],
                                          start=(c == 0), stop=(c == HC - 1))
                mm.then_inc(ey_done, 1)

            def expert_back(e):
                pe.wait_ge(yT_saved, e + 1)
                for a in range(2):
                    mm = nc.tensor.transpose(ps[0:CAPH, 6 + e % 2, a * DM:(a + 1) * DM], yT[:, e % 2, a * CAPH:(a + 1) * CAPH], ident[:])
                mm.then_inc(y_turned, 1)

            pe.wait_ge(logits_saved, CHUNKS)
            pe.wait_ge(slots_ready, 2)
            expert_rows(0)
            for e in range(EXPERTS):
                if e + 1 < EXPERTS:
                    expert_rows(e + 1)
                expert_up(e)
                if e:
                    expert_down(e - 1)
                if e >= 2:
                    expert_back(e - 2)
            expert_down(EXPERTS - 1)
            expert_back(EXPERTS - 2)
            expert_back(EXPERTS - 1)

            pe.wait_ge(relu_done, 2 * EXPERTS)
            pe.wait_ge(y_saved, EXPERTS)
            pe.wait_ge(late_in, 16 * 6)
            turn_rows("qkv1", 0)
            product("qkv1", 0)
            turn_rows("qkv1", 1)
            turn_rows("qkv1", 2)
            product("qkv1", 1)
            turn_rows("qkv1", 3)
            product("qkv1", 2)
            product("qkv1", 3)
            pe.wait_ge(rope_in, 4 * CHUNKS)
            pe.wait_ge(v_saved[1], TILES)
            attention1()
            pe.wait_ge(ff_in, 16 * 4)
            walk(OUT1[1:])

        @block.vector
        def _(dve):
            first = 0

            def row_stats(n, c):
                for t in range(c * CH, (c + 1) * CH):
                    last = nc.vector.bn_stats(stats[:, t, :], x_sb[:, t, :])
                last.then_inc(stats_done, 1)
                dve.wait_ge(stats_done, n * CHUNKS + c + 1)
                for t in range(c * CH, (c + 1) * CH):
                    nc.vector.bn_aggr(ln_mv[:, t, :], stats[:, t, :]).then_inc(ln_step, 1)
                dve.wait_ge(ln_step, (CH + 1) * (n * CHUNKS + c) + CH)
                cs = slice(c * CH, (c + 1) * CH)
                nc.vector.tensor_scalar(ln_ve[:, cs], ln_mv[:, cs, 1], EPS, None, ALU.add).then_inc(ln_step, 1)

            def normalize(n, c):
                dve.wait_ge(rstd_done, n * CHUNKS + c + 1)
                for t in range(c * CH, (c + 1) * CH):
                    nc.vector.tensor_scalar(xn_all[:, t, :], x_sb[:, t, :], ln_mv[:, t, 0:1], ln_rstd[:, t:t + 1],
                                            ALU.subtract, ALU.mult).then_inc(normed, 1)

            def save_v(L, c, count):
                dve.wait_ge(proj_done[L], count)
                v = ps_v if L else ps_qkv0(c)[2]
                for t in range(CH):
                    dst = v_all[:, c * CH + t].rearrange("p g (j d) -> p g j d", d=HV)[:, :, :, 0:HD]
                    nc.vector.tensor_tensor(dst, v[:, t * P:(t + 1) * P].rearrange("p (g j d) -> p g j d", g=GROUPS, j=JH),
                                            bv_b[L][:].rearrange("p (g j d) -> p g j d", g=GROUPS, j=JH), ALU.add).then_inc(v_saved[L], 1)

            def save_kv0(c):
                dve.wait_ge(proj_done[0], 3 * c + 2)
                nc.vector.tensor_scalar(qk_all[:, 1, c * CT:(c + 1) * CT], ps_qkv0(c)[1], bqk[0][:, 1:2], None, ALU.add).then_inc(k_saved[0], 1)
                save_v(0, c, 3 * c + 3)

            def save_kv1(c):
                save_v(1, c, 5 * c + 5)
                rotate(nc.vector, dve, c, 1, rope_step_k, k_saved[1])

            def top_half(it, hp, done=None):
                n = 2 * it + hp
                dve.wait_ge(scores_saved, n + 1)
                if it is not first:
                    dve.wait_ge(masked, 4 * (n - 1))
                dve.sem_inc(top_step, 1)
                k = 1
                for r in range(ROUNDS):
                    src = rest if r else s_sb[:, hp]
                    last = r == ROUNDS - 1
                    for u in range(4):
                        if r:
                            dve.wait_ge(top_step, k - 3 + u * last)
                        nc.vector.max(top[:, hp, u, 8 * r:8 * r + 8], src[:, u, :]).then_inc(tops_done if last else top_step, 1)
                        k += not last
                    if r == 1 and done is not None:
                        contexts(0, done)
                    if not last:
                        for u in range(4):
                            if r == 0 and u == 2:
                                dve.wait_ge(top_step, k - 2)
                                nc.vector.tensor_scalar(peak[:, hp], top[:, hp, :, 0], 1 / MASKED, None, ALU.mult).then_inc(peak_done, 1)
                            dve.wait_ge(top_step, k - 3)
                            nc.vector.match_replace(rest[:, u, :], top[:, hp, u, 8 * r:8 * r + 8], src[:, u, :], NEG).then_inc(top_step, 1)
                            k += 1
                dve.wait_ge(top_step, k)
                dve.sem_clear(top_step)

            def max_half(it, hp):
                s = ps_scores(hp)
                dve.wait_ge(scores_done[1], 2 * it + hp + 1)
                nc.vector.tensor_reduce(row_max[:, :, hp], s, AX_X, ALU.max).then_inc(max_done, 1)
                dve.wait_ge(max_done, 2 * it + hp + 1)
                nc.vector.tensor_scalar(negm[:, hp, :], row_max[:, :, hp], -SCALE, None, ALU.mult).then_inc(neg_done, 1)

            def reciprocals(L, it):
                dve.wait_ge(ctx_T[L], it + 1)
                v = ps_ctx.rearrange("p (q j d) -> p q j d", q=KT, j=JH)
                nc.vector.reciprocal(recip[:], v[:, :, :, HD]).then_inc(recip_done[L], 1)

            def contexts(L, it):
                b, g = it // GROUPS, it % GROUPS
                v = ps_ctx.rearrange("p (q j d) -> p q j d", q=KT, j=JH)
                dve.wait_ge(recip_done[L], it + 1)
                dst = xn_all[:, bass.ds(b * KT, KT), bass.ds(g * JH * HD, JH * HD)].rearrange("p q (j d) -> p q j d", d=HD)
                nc.vector.tensor_tensor(dst, v[:, :, :, 0:HD], recip[:].unsqueeze(3).to_broadcast([P, KT, JH, HD]), ALU.mult)\
                    .then_inc(ctx_done[L], 1)

            def attention0():
                for n in range(2 * LEAD):
                    top_half(n // 2, n % 2)
                    if 1 <= n - 1 < CHUNKS:
                        save_kv0(n - 1)
                    if 1 <= n < CHUNKS:
                        normalize(0, n)
                    if n + 2 < CHUNKS:
                        dve.wait_ge(x_in[n + 2], 16)
                        row_stats(0, n + 2)

                def step(it):
                    top_half(it, 0)
                    reciprocals(0, it - OUT_LAG)
                    top_half(it, 1, it - OUT_LAG)

                for c, (start, end) in enumerate(LOOPS):
                    with dve.Fori(start, end) as it:
                        step(it)
                    top_half(end, 0)
                    reciprocals(0, end - OUT_LAG)
                    if c:
                        normalize(1, c - 1)
                    top_half(end, 1, end - OUT_LAG)
                    if c < len(OUT_AT):
                        step(end + 1)
                        add_attention(0, c)
                dve.wait_ge(tops_done, 4 * 2 * ITERS)
                dve.wait_ge(masked, 4 * (2 * ITERS - 1))
                dve.wait_ge(probs_T[0], 2 * (2 * ITERS - 2))
                for u in range(4):
                    mask_unit(nc.vector, 1, u)
                for it in range(ITERS - OUT_LAG, ITERS):
                    reciprocals(0, it)
                    contexts(0, it)

            def save_pt(it, hp):
                n = 2 * it + hp
                dve.wait_ge(probs_T[1], 2 * n + 2)
                if it is not first:
                    dve.wait_ge(pv_done[1], n - 1)
                nc.vector.tensor_copy(pt_sb[:, hp, 1].rearrange("p a n -> p (a n)"), ps[:, 5, :]).then_inc(pt_done_v, 1)

            def attention1():
                max_half(first, 0)
                max_half(first, 1)
                max_half(1, 0)
                save_pt(first, 0)
                max_half(1, 1)
                save_pt(first, 1)
                with dve.Fori(2, ITERS) as it:
                    max_half(it, 0)
                    save_pt(it - 1, 0)
                    max_half(it, 1)
                    reciprocals(1, it - 2)
                    save_pt(it - 1, 1)
                    contexts(1, it - 2)
                save_pt(ITERS - 1, 0)
                save_pt(ITERS - 1, 1)
                add_attention(1, 0)
                for it in (ITERS - 2, ITERS - 1):
                    reciprocals(1, it)
                    contexts(1, it)

            def add_attention(L, c):
                dve.wait_ge(bias_added, (L * CHUNKS) + c + 1)
                dve.wait_ge(out_done[L], c + 1)
                xs = x_sb[:, c * CH:(c + 1) * CH, :]
                nc.vector.tensor_tensor(xs, xs, ps_out(L).rearrange("p (t d) -> p t d", d=DM), ALU.add).then_inc(res_done[L], 1)
                dve.wait_ge(res_done[L], c + 1)
                row_stats(2 * L + 1, c)

            nc.vector.memset(ones_b[:], 1.0).then_inc(setup_dve, 1)
            nc.vector.memset(zero_rows[:], 0.0).then_inc(setup_dve, 1)
            dve.wait_ge(x_in[0], 16)
            row_stats(0, 0)
            normalize(0, 0)
            dve.wait_ge(consts_in, 16 * 7)
            dve.wait_ge(x_in[1], 16)
            row_stats(0, 1)
            save_kv0(0)
            attention0()
            dve.wait_ge(route_in, 16 * 4)
            nc.vector.tensor_copy(triu_b[:], triu[:]).then_inc(setup_dve, 1)
            add_attention(0, CHUNKS - 1)
            normalize(1, CHUNKS - 1)

            steps = [0]

            def step(ins):
                ins.then_inc(rstep, 1)
                steps[0] += 1
                dve.wait_ge(rstep, steps[0])

            def col(a):
                return a.unsqueeze(2).to_broadcast([P, TILES, EXPERTS])

            lmax, who, esum, prob, place, keep, slot, tmp, weight = (rs[:, i, :] for i in range(9))
            dve.wait_ge(logits_saved, CHUNKS)
            step(nc.vector.tensor_reduce(lmax, logits[:], AX_X, ALU.max))
            step(nc.vector.tensor_tensor(rt[:, 0], logits[:], col(lmax), ALU.subtract))
            step(nc.vector.tensor_scalar(rt[:, 2], rt[:, 0], 0.0, None, ALU.is_ge))
            step(nc.vector.tensor_tensor(rt[:, 2], rt[:, 2], rev[:], ALU.mult))
            step(nc.vector.tensor_reduce(who, rt[:, 2], AX_X, ALU.max))
            step(nc.vector.tensor_tensor(rt[:, 3], rt[:, 2], col(who), ALU.is_equal))
            nc.vector.tensor_copy(mask_b[:], rt[:, 3]).then_inc(mask_done, 1)
            dve.wait_ge(gate_exp, 1)
            step(nc.vector.tensor_reduce(esum, rt[:, 1], AX_X, ALU.add))
            step(nc.vector.reciprocal(prob, esum))
            dve.wait_ge(cum_done, 1)
            step(nc.vector.tensor_tensor(rt[:, 0], rt[:, 3], ps[:, 6, 0:ER].rearrange("p (t e) -> p t e", e=EXPERTS), ALU.mult))
            step(nc.vector.tensor_reduce(place, rt[:, 0], AX_X, ALU.add))
            step(nc.vector.tensor_scalar(keep, place, float(CAP), None, ALU.is_le))
            step(nc.vector.tensor_scalar(tmp, who, -float(CAP), float(EXPERTS * CAP - 1), ALU.mult, ALU.add))
            step(nc.vector.tensor_tensor(slot, tmp, place, ALU.add))
            step(nc.vector.tensor_tensor(tmp, slot, spill[:], ALU.subtract))
            step(nc.vector.tensor_tensor(tmp, tmp, keep, ALU.mult))
            nc.vector.tensor_tensor(slot_idx[:], tmp, spill[:], ALU.add).then_inc(slots_ready, 1)
            nc.vector.tensor_tensor(back_idx[:], slot, keep, ALU.mult).then_inc(slots_ready, 1)
            step(nc.vector.tensor_tensor(weight, prob, keep, ALU.mult))

            def clear_slot(e):
                dve.wait_ge(ey_done, e + 1)
                for w in (w1_ring, w2_ring):
                    nc.vector.memset(w[STACK // 32 * 32:P, e % RING], 0.0).then_inc(stack_zeroed, 1)

            for e in range(EXPERTS):
                for bank in range(2):
                    dve.wait_ge(eh_done, 2 * e + bank + 1)
                    if e >= 2:
                        dve.wait_ge(ey_done, e - 1)
                    nc.vector.tensor_scalar(ehT[:, e % 2, 2 * bank:2 * bank + 2, :].rearrange("p c n -> p (c n)"),
                                            ps[:, 2 + 2 * (e % 2) + bank, 0:2 * CAP], 0.0, None, ALU.max).then_inc(relu_done, 1)
                if e >= RING + 2:
                    clear_slot(e - 2)
            clear_slot(EXPERTS - 2)
            clear_slot(EXPERTS - 1)

            def add_moe(c):
                dve.wait_ge(gathered[c], 16 * CH)
                for t in range(c * CH, (c + 1) * CH):
                    nc.vector.scalar_tensor_tensor(out=x_sb[:, t, :], in0=xn_all[:, t, :], scalar=weight[:, t:t + 1], in1=x_sb[:, t, :],
                                                   op0=ALU.mult, op1=ALU.add).then_inc(moe_added, 1)
                dve.wait_ge(moe_added, CH * (c + 1))
                row_stats(2, c)

            for c in range(CHUNKS + 3):
                if c < CHUNKS:
                    add_moe(c)
                if 1 <= c <= CHUNKS:
                    normalize(2, c - 1)
                if c == 2:
                    dve.wait_ge(late_in, 16 * 6)
                if c >= 3:
                    save_kv1(c - 3)
            attention1()
            dve.wait_ge(ff_in, 16 * 4)

            def save_hidden(c):
                for i in range(2, HC):
                    dve.wait_ge(h_done, HC * c + i + 1)
                    nc.vector.tensor_scalar(hT[:, c % 2, i, :], ps[:, 4 + i, :], ffb1_sb[:, i:i + 1], 0.0, ALU.add, ALU.max).then_inc(h_saved_v, 1)

            def add_mlp(c):
                dve.wait_ge(bias_added, 2 * CHUNKS + c + 1)
                dve.wait_ge(ff_done, c + 1)
                xs = x_sb[:, c * CH:(c + 1) * CH, :]
                nc.vector.tensor_tensor(xs, xs, ps_down.rearrange("p (t d) -> p t d", d=DM), ALU.add).then_inc(added, 1)

            for c in range(CHUNKS + 3):
                if 1 <= c <= CHUNKS:
                    normalize(3, c - 1)
                if 1 <= c < CHUNKS:
                    add_attention(1, c)
                if 2 <= c <= CHUNKS + 1:
                    save_hidden(c - 2)
                if c >= 3:
                    add_mlp(c - 3)


def kernel(**inputs):
    import numpy as np
    import concourse.bacc as bacc
    from concourse.bass_utils import run_bass_kernel_spmd

    a = {k: np.asarray(v) for k, v in inputs.items()}
    f32 = np.float32
    swap = np.arange(DM) ^ 1

    def columns(*rows):
        return np.ascontiguousarray(np.stack(rows, axis=1))

    d = np.arange(DM) % HD
    inv_freq = (f32(1.0) / f32(10000.0) ** (np.arange(0, HD, 2, dtype=f32) / f32(HD))).astype(f32)
    angle = (inv_freq[d % (HD // 2)][:, None] * np.tile(np.arange(SEQ, dtype=f32), CT // SEQ)[None, :]).astype(f32)
    sign = np.where(d % 2 == 0, f32(-1), f32(1))[:, None]
    token = np.arange(TILES, dtype=f32)[None, :] * P + np.arange(P, dtype=f32)[:, None]
    arrays = {
        "x": a["L0_attn_x"],
        "w0": columns(*(a[f"L0_attn_W{n}"].T for n in "qkvo")),
        "bqk0": columns(a["L0_attn_bq"], a["L0_attn_bk"]),
        "bv0": a["L0_attn_bv"],
        "bo0": a["L0_attn_bo"],
        "gate": a["L0_ffn_gate_w"].T,
        "w1": a["L0_ffn_w1"],
        "w2": a["L0_ffn_w2"],
        "w5": columns(*(a[f"L1_attn_W{n}"].T for n in "qkvo"), a["L1_attn_Wq"][swap].T, a["L1_attn_Wk"][swap].T),
        "bqk1": columns(a["L1_attn_bq"], a["L1_attn_bk"], a["L1_attn_bq"][swap], a["L1_attn_bk"][swap]),
        "bv1": a["L1_attn_bv"],
        "bo1": a["L1_attn_bo"],
        "ffw1": a["L1_ffn_W1"],
        "ffb1": a["L1_ffn_b1"].reshape(HC, P).T,
        "ffw2": a["L1_ffn_W2"],
        "ffb2": a["L1_ffn_b2"],
        "ident_d": np.eye(P, dtype=f32),
        "neg_ident_d": np.eye(P, dtype=f32) * f32(-MASKED),
        "hmask_d": (np.arange(DM)[:, None] // HD == np.arange(HEADS)[None, :]).astype(f32),
        "cos_d": np.cos(angle).astype(f32),
        "sin_d": (sign * np.sin(angle)).astype(f32),
        "triu_d": np.triu(np.ones((P, P), dtype=f32)),
        "rev_d": np.broadcast_to(EXPERTS - np.arange(EXPERTS, dtype=f32), (P, TILES, EXPERTS)),
        "spill_d": token + f32(SLOTS),
    }
    arrays = {k: np.ascontiguousarray(v) for k, v in arrays.items()}
    nc = bacc.Bacc("TRN2", target_bir_lowering=False, num_devices=1)
    args = {k: nc.dram_tensor(f"in_{k}", v.shape, F32, kind="ExternalInput").ap() for k, v in arrays.items()}
    out = nc.dram_tensor("out_0", (BATCH, SEQ, DM), F32, kind="ExternalOutput").ap()
    build(nc, out=out, **args)
    r = run_bass_kernel_spmd(nc, [{f"in_{k}": v for k, v in arrays.items()}], core_ids=[0])
    return r.results[0]["out_0"]
```
